# Optimizing a Trainium2 kernel written in Bass

```python
import numpy as np
import jax
import jax.numpy as jnp

def _softmax(x, axis=-1):
    return jax.nn.softmax(x, axis=axis)

def _gelu(x):
    return jax.nn.gelu(x, approximate=True)

def _silu(x):
    return jax.nn.silu(x)

def _sigmoid(x):
    return jax.nn.sigmoid(x)

def _layernorm(x, axis=-1, eps=1e-05):
    m = jnp.mean(x, axis=axis, keepdims=True)
    v = jnp.var(x, axis=axis, keepdims=True)
    return (x - m) / jnp.sqrt(v + eps)

def _scatter_add(tgt, idx, src, axis=0):
    return tgt.at[idx].add(src)

def _segment_sum(src, seg, n):
    return jax.ops.segment_sum(src, seg, n)
kernel_name = 'mk_adaln_ffn_d1_seqx_r8_7691d2'

def setup_inputs(seed: int=0):
    np.random.seed(seed)
    _w = jnp.asarray

    def _rec_inputs():
        import jax
        import jax.numpy as jnp
        _rk = jax.random.key(seed)
        x = 7.22e-05 + 1 * jax.random.normal(jax.random.fold_in(_rk, 1), (16, 128, 256), jnp.float32)
        _lenS = 128 - jax.random.randint(jax.random.fold_in(_rk, 7), (16,), 0, max(1, 128 // 4) + 1, jnp.int32)
        _lenS2 = 128 - jax.random.randint(jax.random.fold_in(_rk, 8), (16,), 0, max(1, 128 // 4) + 1, jnp.int32)
        cond_2048 = jax.random.bernoulli(jax.random.fold_in(_rk, 11), 0.5063, (16, 256)).astype(jnp.float32)
        return (x, cond_2048)
    x, cond_2048 = _rec_inputs()

    def _L0_cond_setup():
        import jax, jax.numpy as jnp
        import numpy as np
        NH = 8
        NEG = -1e+30
        key = jax.random.key(seed)
        k1, k2, k3, k4 = jax.random.split(key, 4)
        B, D, T = (4, 128, 256)
        x = jax.random.normal(k1, (B, D, T), dtype=jnp.float32)
        mask = jax.random.randint(k2, (B, T), 0, 2).astype(jnp.float32)
        lim = float(np.sqrt(6.0 / (D + D)))
        Wq = jax.random.uniform(k3, (D, D), dtype=jnp.float32, minval=-lim, maxval=lim)
        Wo = jax.random.uniform(k4, (D, D), dtype=jnp.float32, minval=-lim, maxval=lim)
        return {'x': x, 'mask': mask, 'Wq': Wq, 'Wo': Wo}
    _L0_cond_all = _L0_cond_setup()
    _L0_cond_in = {k: v for k, v in _L0_cond_all.items() if k in ('Wq', 'Wo')}
    del _L0_cond_all

    def _L0_ffn_setup():
        import jax, jax.numpy as jnp
        import numpy as np

        @jax.custom_vjp
        def ste_sign(x):
            return jnp.sign(x)

        def _ste_fwd(x):
            return (jnp.sign(x), None)

        def _ste_bwd(_, g):
            return (g,)
        ste_sign.defvjp(_ste_fwd, _ste_bwd)
        D_MODEL = 256
        D_HIDDEN = 1024
        key = jax.random.key(seed)
        k_x, k_up, k_dn = jax.random.split(key, 3)
        x = jax.random.normal(k_x, (2, 256, D_MODEL), dtype=jnp.float32)
        up_weight = jax.random.normal(k_up, (D_HIDDEN, D_MODEL), dtype=jnp.float32) * 0.02
        down_weight = jax.random.normal(k_dn, (D_MODEL, D_HIDDEN), dtype=jnp.float32) * 0.02
        up_scale = jnp.ones((D_HIDDEN,), dtype=jnp.float32)
        down_scale = jnp.ones((D_MODEL,), dtype=jnp.float32)
        output_scale = jnp.ones((1,), dtype=jnp.float32)
        return {'x': x, 'up_weight': up_weight, 'down_weight': down_weight, 'up_scale': up_scale, 'down_scale': down_scale, 'output_scale': output_scale}
    _L0_ffn_all = _L0_ffn_setup()
    _L0_ffn_in = {k: v for k, v in _L0_ffn_all.items() if k in ('up_weight', 'down_weight', 'up_scale', 'down_scale', 'output_scale')}
    del _L0_ffn_all
    return {'x': x, 'cond_2048': cond_2048, 'L0_cond_Wq': _L0_cond_in['Wq'], 'L0_cond_Wo': _L0_cond_in['Wo'], 'L0_ffn_up_weight': _L0_ffn_in['up_weight'], 'L0_ffn_down_weight': _L0_ffn_in['down_weight'], 'L0_ffn_up_scale': _L0_ffn_in['up_scale'], 'L0_ffn_down_scale': _L0_ffn_in['down_scale'], 'L0_ffn_output_scale': _L0_ffn_in['output_scale']}

def reference(x, cond_2048, L0_cond_Wq, L0_cond_Wo, L0_ffn_up_weight, L0_ffn_down_weight, L0_ffn_up_scale, L0_ffn_down_scale, L0_ffn_output_scale):
    import jax
    import jax.numpy as jnp

    def _L0_cond_ref(x, mask, Wq, Wo):
        import jax, jax.numpy as jnp
        import numpy as np
        NH = 8
        NEG = -1e+30
        B, D, T = x.shape
        dk = D // NH
        scale = 1.0 / jnp.sqrt(jnp.asarray(dk, x.dtype))
        xt = jnp.transpose(x, (0, 2, 1))
        q = xt @ Wq.T
        qh = q.reshape(B, T, NH, dk).transpose(0, 2, 1, 3)
        scores = scale * jnp.einsum('bhqd,bhkd->bhqk', qh, qh)
        cmask = mask[:, None, None, :]
        rmask = mask[:, None, :, None]
        logits = (scores * cmask + (1.0 - cmask) * NEG) * rmask
        attn = jax.nn.softmax(logits, axis=-1)
        ctx = jnp.einsum('bhqk,bhkd->bhqd', attn, qh)
        ctx = ctx.transpose(0, 2, 1, 3).reshape(B, T, D)
        out = ctx @ Wo.T
        return jnp.transpose(out, (0, 2, 1))

    def _L0_ffn_ref(x, up_weight, down_weight, up_scale, down_scale, output_scale):
        import jax, jax.numpy as jnp
        import numpy as np

        @jax.custom_vjp
        def ste_sign(x):
            return jnp.sign(x)

        def _ste_fwd(x):
            return (jnp.sign(x), None)

        def _ste_bwd(_, g):
            return (g,)
        ste_sign.defvjp(_ste_fwd, _ste_bwd)
        D_MODEL = 256
        D_HIDDEN = 1024
        up_w = ste_sign(up_weight)
        down_w = ste_sign(down_weight)
        hidden = jnp.einsum('bsd,hd->bsh', x, up_w) * up_scale
        hidden = jax.nn.relu(hidden)
        out = jnp.einsum('bsh,dh->bsd', hidden, down_w) * down_scale
        return out * output_scale
    x = x + _L0_ffn_ref(_L0_cond_ref(x, cond_2048, L0_cond_Wq, L0_cond_Wo), L0_ffn_up_weight, L0_ffn_down_weight, L0_ffn_up_scale, L0_ffn_down_scale, L0_ffn_output_scale)
    return x

_drawn_inputs = setup_inputs


def setup_inputs(seed=0):
    import zlib

    import numpy as np

    out = dict(_drawn_inputs(seed))
    spreads = {'L0_ffn_up_scale': (1.0, 0.2), 'L0_ffn_down_scale': (1.0, 0.2)}
    factors = {}
    for name, (base, spread) in spreads.items():
        noise = np.random.default_rng([zlib.crc32(name.encode()), seed]).standard_normal(out[name].shape)
        drawn = base * np.exp(spread * noise) if base else spread * noise
        out[name] = jnp.asarray(drawn.astype(out[name].dtype))
    for name, factor in factors.items():
        out[name] = (out[name] * factor).astype(out[name].dtype)
    return out
```

```python
from contextlib import ExitStack

import concourse.bass as bass
from concourse import mybir

F32 = mybir.dt.float32
F32R = mybir.dt.float32r
BF16 = mybir.dt.bfloat16
ACT = mybir.ActivationFunctionType
ALU = mybir.AluOpType
AX_X = mybir.AxisListType.X

B, D, T = 16, 128, 256
NH = 8
DK = D // NH
HID = 1024
P = 128
TT = T // P
HT = HID // P
HALF = NH // 2
SCALE = DK ** -0.5
NEG = -1e30 / SCALE
BLOCKS = 2 * T // 32
RING = 4

ROW_MID, ROW_HI, ROW_R, ROW_LO, ROW_NEG = 0, DK, 2 * DK, 2 * DK + 1, 3 * DK + 1
ROWS = 3 * DK + 2
K_MASKED = 6 * DK + 1
K_ALL = K_MASKED + 2


class Slot:

    def __init__(self, turn, j):
        self.turn, self.j = turn, j
        self.b = turn * RING + (2 + j)
        self.odd = j % 2 == 1
        self.pair = turn * 2 + j // 2
        self.pair_buf = (j // 2) % 2

    def batch(self, d):
        n = 2 + self.j + d
        return self.turn * RING + n, n % RING, self.turn + n // RING


def attention_ffn(nc, x, mask, wq_by_head, wq_by_dim, wo_t, up_t, down_t, up_scale, down_scale,
                  output_scale, out):
    parts = nc.dram_tensor("parts_dram", (B, ROWS, NH * T), BF16, kind="Internal").ap()
    ctx = ExitStack()
    with ctx:
        def sb(name, shape, dt=F32):
            return ctx.enter_context(nc.sbuf_tensor(name, shape, dt))

        def pb(name):
            return ctx.enter_context(nc.psum_tensor(name, [P, 512], F32))

        def sem(name):
            return ctx.enter_context(nc.semaphore(name))

        x_all = sb("x_all", [P, B, T])
        mask_all = sb("mask_all", [P, B, T])
        out_all = sb("out_all", [P, B, T])
        wq_h = sb("wq_h", [P, D])
        wq_d = sb("wq_d", [P, D])
        wo_pad = sb("wo_pad", [P, 2, D])
        up_raw = sb("up_raw", [P, TT, HID])
        down_raw = sb("down_raw", [P, HT, T])
        up_sign = sb("up_sign", [P, TT, HID], F32R)
        down_sign = sb("down_sign", [P, HT, T], F32R)
        up_sc = sb("up_sc", [P, HT])
        down_sc = sb("down_sc", [P, T])
        out_sc = sb("out_sc", [P, 1])
        out_scale = sb("out_scale", [P, T])
        ident = sb("ident", [P, P], BF16)
        mask16 = sb("mask16", [B, T])
        r16 = sb("r16", [B, T], BF16)
        neg16 = sb("neg16", [B, T], BF16)
        x_masked = [sb(f"x_masked{i}", [P, T]) for i in range(2)]
        x_copy = [sb(f"x_copy{i}", [P, T]) for i in range(2)]
        q_parts = [sb(f"q_parts{i}", [P, 3, T], BF16) for i in range(2)]
        q_rest = sb("q_rest", [P, T])
        key_stack = [sb(f"key_stack{i}", [P, NH, T], BF16) for i in range(RING)]
        query_stack = [sb(f"query_stack{i}", [P, NH, T], BF16) for i in range(RING)]
        v_ones = [sb(f"v_ones{i}", [P, TT, NH, 32]) for i in range(RING)]
        maxima = sb("maxima", [P, 2, HALF, TT])
        neg_max = sb("neg_max", [P, 2, 2, HALF * TT], BF16)
        neg_max_rows = [sb(f"neg_max_rows{i}", [2 * HALF * TT, P], BF16) for i in range(2)]
        probs = sb("probs", [P, NH, TT * T])
        turned_context = sb("turned_context", [P, 2 * T])
        inverse_sums = sb("inverse_sums", [P, BLOCKS])
        normal_context = sb("normal_context", [P, 2 * T])
        context = sb("context", [P, 2, T])
        o_hi = [sb(f"o_hi{i}", [P, TT, 2, D], F32R) for i in range(2)]
        o_lo = [sb(f"o_lo{i}", [P, TT, 2, D], F32R) for i in range(2)]
        hidden = sb("hidden", [P, HT, 2 * D])
        hid_hi = sb("hid_hi", [P, HT, 2 * D], F32R)
        hid_lo = sb("hid_lo", [P, HT, 2 * D], F32R)

        ps_exp = [pb(f"ps_exp{i}") for i in range(2)]
        ps_max = [pb(f"ps_max{i}") for i in range(2)]
        ps_ctx = pb("ps_ctx")
        ps_proj = pb("ps_proj")
        ps_up = pb("ps_up")
        ps_down = pb("ps_down")
        ps_neg_max = ps_proj[0:2 * HALF * TT, 0:P // 2].bitcast(BF16)

        weights_loaded, wo_loaded = sem("weights_loaded"), sem("wo_loaded")
        x_first, x_rest = sem("x_first"), sem("x_rest")
        mask_loaded, mask_stored = sem("mask_loaded"), sem("mask_stored")
        ffn_loaded, scales_loaded = sem("ffn_loaded"), sem("scales_loaded")
        parts_stored = sem("parts_stored")
        stack_loaded = [sem(f"stack_loaded{i}") for i in range(RING)]
        max_loaded = [sem(f"max_loaded{i}") for i in range(2)]
        out_stored = sem("out_stored")
        zeroed, constants_set = sem("zeroed"), sem("constants_set")
        ident_zeroed, ident_made = sem("ident_zeroed"), sem("ident_made")
        x_masked_ready, x_prepared = sem("x_masked_ready"), sem("x_prepared")
        hid_lo_done, out_ready = sem("hid_lo_done"), sem("out_ready")
        projected, max_scored, exp_scored = sem("projected"), sem("max_scored"), sem("exp_scored")
        max_turned, attended, out_projected = sem("max_turned"), sem("attended"), sem("out_projected")
        up_done, down_done = sem("up_done"), sem("down_done")
        signs_made = sem("signs_made")
        q_hi_done, v_done, max_copied = sem("q_hi_done"), sem("v_done"), sem("max_copied")
        exp_done, o_hi_done, relu_done = sem("exp_done"), sem("o_hi_done"), sem("relu_done")
        mask_rows_made = sem("mask_rows_made")
        scale_made = sem("scale_made")
        q_rest_done, q_mid_done, q_lo_done = sem("q_rest_done"), sem("q_mid_done"), sem("q_lo_done")
        maxed, max_hi_done, max_split = sem("maxed"), sem("max_hi_done"), sem("max_split")
        context_turned, inverted, normalised = sem("context_turned"), sem("inverted"), sem("normalised")
        context_done, o_lo_done = sem("context_done"), sem("o_lo_done")
        hid_hi_done, scaled = sem("hid_hi_done"), sem("scaled")

        block = ctx.enter_context(nc.Block())

        def pipeline(engine, first, slot, last):
            first()
            for j in (-2, -1):
                slot(Slot(0, j), attends_before=j == -1, ffn=False, ahead1=True, ahead2=True)
            with engine.Fori(0, (B - RING) // RING) as turn:
                for j in range(RING):
                    slot(Slot(turn, j), attends_before=True, ffn=True, ahead1=True, ahead2=True)
            for j in (0, 1):
                slot(Slot((B - RING) // RING, j), attends_before=True, ffn=True, ahead1=j == 0, ahead2=False)
            last()

        @block.sync
        def _(sp):
            def load_parts(b, r):
                def rows(at, n, twice=False):
                    src = parts[b, at:at + n, :]
                    if twice:
                        src = bass.AP(src.tensor, src.offset, [[0, 2], [NH * T, n], [1, NH * T]])
                    return src
                key, query, done = key_stack[r], query_stack[r], stack_loaded[r]
                sp.dma_start(key[0:2 * DK, :, :], rows(ROW_MID, DK, True)).then_inc(done, 16)
                sp.dma_start(query[0:4 * DK, :, :], rows(ROW_MID, 2 * DK, True)).then_inc(done, 16)
                sp.dma_start(key[2 * DK:4 * DK, :, :], rows(ROW_HI, DK, True)).then_inc(done, 16)
                sp.dma_start(key[4 * DK:5 * DK, :, :], rows(ROW_HI, DK)).then_inc(done, 16)
                sp.dma_start(query[4 * DK:5 * DK, :, :], rows(ROW_LO, DK)).then_inc(done, 16)
                sp.dma_start(key[5 * DK:K_MASKED, :, :], rows(ROW_LO, DK + 1)).then_inc(done, 16)
                sp.dma_start(query[5 * DK:K_MASKED, :, :], rows(ROW_HI, DK + 1)).then_inc(done, 16)

            def store_parts(b, i):
                dst = parts[b, 0:2 * DK, :].rearrange("(s d) (h t) -> (d h) s t", s=2, h=NH)
                sp.wait_ge(q_hi_done, b + 1)
                sp.wait_ge(q_mid_done, b + 1)
                sp.dma_start(dst, q_parts[i][:, 0:2, :]).then_inc(parts_stored, 16)
                dst = parts[b, ROW_LO:ROW_LO + DK, :].rearrange("d (h t) -> (d h) t", h=NH)
                sp.wait_ge(q_lo_done, b + 1)
                sp.dma_start(dst, q_parts[i][:, 2, :]).then_inc(parts_stored, 16)

            def load_maxima(b, r, half):
                sp.wait_ge(max_copied, b * 2 + (half + 1))
                sp.dma_start(query_stack[r][K_MASKED:K_ALL, half * HALF:(half + 1) * HALF, :],
                             neg_max_rows[half][:, :]).then_inc(max_loaded[half], 16)

            def first():
                sp.dma_start(x_all[:, 0:2, :], x[0:2].rearrange("b p t -> p b t")).then_inc(x_first, 16)
                sp.dma_start(mask_all[:, 0:2, :], mask[0:2, :].partition_broadcast(P)).then_inc(x_first, 16)
                sp.dma_start(mask16[:, :], mask).then_inc(mask_loaded, 16)
                sp.dma_start(wq_h[:, :], wq_by_head).then_inc(weights_loaded, 16)
                sp.dma_start(wq_d[:, :], wq_by_dim).then_inc(weights_loaded, 16)
                sp.wait_ge(mask_rows_made, 1)
                for row, rows in ((ROW_R, r16), (ROW_NEG, neg16)):
                    for h in range(NH):
                        sp.dma_start(parts[:, row, h * T:(h + 1) * T], rows[:, :]).then_inc(mask_stored, 16)
                sp.wait_ge(mask_stored, 2 * NH * 16)
                for b in range(2):
                    store_parts(b, b)
                    sp.wait_ge(parts_stored, 32 * (b + 1))
                    if b == 0:
                        sp.wait_ge(constants_set, 1)
                    load_parts(b, b)
                sp.dma_start(x_all[:, 2:B, :], x[2:B].rearrange("b p t -> p b t")).then_inc(x_rest, 16)
                sp.dma_start(mask_all[:, 2:B, :], mask[2:B, :].partition_broadcast(P)).then_inc(x_rest, 16)
                load_maxima(0, 0, 0)
                sp.wait_ge(zeroed, 1)
                for j in range(HALF):
                    sp.dma_start(wo_pad[32 * j:32 * j + DK, :, :],
                                 wo_t.rearrange("(g j d) o -> j d g o", g=2, j=HALF)[j]).then_inc(wo_loaded, 16)
                sp.dma_start(up_raw[:, :, :], up_t.rearrange("(k p) n -> p k n", p=P)).then_inc(ffn_loaded, 16)
                sp.dma_start(down_raw[:, :, :], down_t.rearrange("(k p) n -> p k n", p=P)).then_inc(ffn_loaded, 16)
                sp.dma_start(up_sc[:, :], up_scale).then_inc(scales_loaded, 16)
                sp.dma_start(down_sc[:, :], down_scale.partition_broadcast(P)).then_inc(scales_loaded, 16)
                sp.dma_start(out_sc[:, :], output_scale.partition_broadcast(P)).then_inc(scales_loaded, 16)

            def store_out(pair):
                sp.wait_ge(out_ready, pair + 1)
                sp.dma_start(out[bass.ds(pair * 2, 2)].rearrange("b p t -> p b t"),
                             out_all[:, bass.ds(pair * 2, 2), :]).then_inc(out_stored, 16)

            def slot(s, attends_before, ffn, ahead1, ahead2):
                b, r, _ = s.batch(0)
                load_maxima(b, r, 1)
                if ahead2:
                    b2, r2, _ = s.batch(2)
                    store_parts(b2, r2 % 2)
                if ahead1:
                    b1, r1, _ = s.batch(1)
                    load_maxima(b1, r1, 0)
                if ahead2:
                    sp.wait_ge(parts_stored, b2 * 32 + 32)
                    load_parts(b2, r2)
                if ffn and s.odd:
                    store_out(s.pair)

            def last():
                store_out(B // 2 - 1)
                sp.wait_ge(out_stored, 16 * (B // 2))

            pipeline(sp, first, slot, last)

        @block.gpsimd
        def _(pool):
            def prepare(b, i):
                nc.gpsimd.tensor_tensor(x_masked[i][:, :], x_all[:, b, :], mask_all[:, b, :],
                                        ALU.mult).then_inc(x_masked_ready, 1)
                nc.gpsimd.tensor_copy(x_copy[i][:, :], x_all[:, b, :]).then_inc(x_prepared, 1)

            def first():
                pool.wait_ge(x_first, 32)
                for b in range(2):
                    prepare(b, b)
                nc.gpsimd.memset(ident[:, :], 0.0).then_inc(ident_zeroed, 1)
                pool.wait_ge(ident_zeroed, 1)
                nc.gpsimd.affine_select(out=ident[:, :], in_=ident[:, :], compare_op=ALU.not_equal, fill=1.0,
                                        base=0, pattern=[[-1, P]], channel_multiplier=1).then_inc(ident_made, 1)
                nc.gpsimd.memset(wo_pad[:, :, :], 0.0).then_inc(zeroed, 1)
                pool.wait_ge(x_rest, 32)

            def hid_low(pair, t):
                pool.wait_ge(hid_hi_done, pair * HT + (t + 1))
                nc.gpsimd.tensor_tensor(hid_lo[:, t, :], hidden[:, t, :], hid_hi[:, t, :],
                                        ALU.subtract).then_inc(hid_lo_done, 1)

            def residual(pair):
                pool.wait_ge(scaled, pair + 1)
                o = out_all[:, bass.ds(pair * 2, 2), :]
                nc.gpsimd.tensor_tensor(o, o, x_all[:, bass.ds(pair * 2, 2), :], ALU.add).then_inc(out_ready, 1)

            def slot(s, attends_before, ffn, ahead1, ahead2):
                if ahead2:
                    b2, r2, _ = s.batch(2)
                    pool.wait_ge(projected, b2 - 1)
                    prepare(b2, r2 % 2)
                if ffn:
                    for t in range(HALF):
                        hid_low(s.pair, t + (HALF if s.odd else 0))
                    if s.odd:
                        residual(s.pair)

            def last():
                for t in range(HT):
                    hid_low(B // 2 - 1, t)
                residual(B // 2 - 1)

            pipeline(pool, first, slot, last)

        @block.tensor
        def _(pe):
            def project(b, i, after_maxima):
                pe.wait_ge(x_masked_ready, b + 1)
                if after_maxima is not None:
                    pe.wait_ge(max_copied, after_maxima)
                nc.tensor.matmul(ps_proj[:, 0:T], wq_d[:, :], x_masked[i][:, :], start=True, stop=True)
                pe.wait_ge(x_prepared, b + 1)
                for t in range(TT):
                    mm = nc.tensor.matmul(ps_proj[:, T + t * D:T + (t + 1) * D], x_copy[i][:, t * P:(t + 1) * P],
                                          wq_h[:, :], start=True, stop=True)
                mm.then_inc(projected, 1)

            def score_max(b, r, uses, h):
                if h == 0:
                    pe.wait_ge(stack_loaded[r], uses * 112 + 112)
                if not (isinstance(b, int) and b == 0 and h < 2):
                    pe.wait_ge(maxed, b * NH + (h - 1))
                for t in range(TT):
                    mm = nc.tensor.matmul(ps_max[h % 2][:, t * T:(t + 1) * T],
                                          query_stack[r][0:K_MASKED, h, t * P:(t + 1) * P],
                                          key_stack[r][0:K_MASKED, h, :], start=True, stop=True)
                mm.then_inc(max_scored, 1)

            def score_exp(b, r, h):
                if h % HALF == 0:
                    pe.wait_ge(max_loaded[h // HALF], b * 16 + 16)
                if not (isinstance(b, int) and b == 0 and h < 2):
                    pe.wait_ge(exp_done, b * NH + (h - 1))
                for t in range(TT):
                    mm = nc.tensor.matmul(ps_exp[h % 2][:, t * T:(t + 1) * T],
                                          key_stack[r][0:K_ALL, h, t * P:(t + 1) * P],
                                          query_stack[r][0:K_ALL, h, :], start=True, stop=True)
                mm.then_inc(exp_scored, 1)

            def turn_maxima(b, half):
                pe.wait_ge(max_split, b * 2 + (half + 1))
                if half == 1:
                    pe.wait_ge(max_copied, b * 2 + 1)
                nc.tensor.transpose(ps_neg_max, neg_max[:, half, :, :].rearrange("p s c -> p (s c)"),
                                    ident[:, :]).then_inc(max_turned, 1)

            def attend(b, r, half):
                pe.wait_ge(exp_done, b * NH + (half + 1) * HALF)
                if half == 0:
                    pe.wait_ge(v_done, b + 1)
                for t in range(TT):
                    for j in range(HALF):
                        h = half * HALF + j
                        mm = nc.tensor.matmul(ps_ctx[32 * j:32 * j + 32, half * T:(half + 1) * T],
                                              v_ones[r][:, t, h, :], probs[:, h, t * T:(t + 1) * T],
                                              start=t == 0, stop=t == TT - 1)
                mm.then_inc(attended, 1)

            def project_out(b):
                pe.wait_ge(context_done, b + 1)
                for t in range(TT):
                    for g in range(2):
                        mm = nc.tensor.matmul(ps_ctx[:, t * D:(t + 1) * D], context[:, g, t * P:(t + 1) * P],
                                              wo_pad[:, g, :], start=g == 0, stop=g == 1)
                mm.then_inc(out_projected, 1)

            def up(pair, i, t):
                if t == 0:
                    pe.wait_ge(o_lo_done, pair * 2 + 2)
                else:
                    pe.wait_ge(relu_done, pair * HT + t)
                for n, (k, part) in enumerate((k, part) for k in range(TT) for part in (o_hi, o_lo)):
                    mm = nc.tensor.matmul(ps_up[:, 0:2 * D], up_sign[:, k, t * P:(t + 1) * P],
                                          part[i][:, k, :, :].rearrange("p b s -> p (b s)"),
                                          start=n == 0, stop=n == 2 * TT - 1)
                mm.then_inc(up_done, 1)

            def down(pair, bi, t):
                if bi == 0:
                    pe.wait_ge(hid_lo_done, pair * HT + (t + 1))
                for part in (hid_hi, hid_lo):
                    mm = nc.tensor.matmul(ps_down[:, bi * T:(bi + 1) * T], part[:, t, bi * D:(bi + 1) * D],
                                          down_sign[:, t, :], start=t == 0 and part is hid_hi,
                                          stop=t == HT - 1 and part is hid_lo)
                if bi == 1 and t == HT - 1:
                    mm.then_inc(down_done, 1)

            def first():
                pe.wait_ge(weights_loaded, 32)
                project(0, 0, None)
                pe.wait_ge(q_rest_done, 1)
                project(1, 1, None)
                pe.wait_ge(ident_made, 1)
                for h in range(NH):
                    score_max(0, 0, 0, h)
                    if h == 5:
                        pe.wait_ge(q_rest_done, 2)
                        turn_maxima(0, 0)
                pe.wait_ge(wo_loaded, 16 * HALF)
                pe.wait_ge(signs_made, 2)

            def slot(s, attends_before, ffn, ahead1, ahead2):
                b, r, uses = s.batch(0)
                for h in range(NH):
                    if h == 0:
                        turn_maxima(b, 1)
                    score_exp(b, r, h)
                    if ahead1:
                        b1, r1, uses1 = s.batch(1)
                        score_max(b1, r1, uses1, h)
                    if h == 0 and attends_before:
                        attend(b - 1, (r - 1) % RING, 1)
                    if h == 1 and ahead2:
                        b2, r2, _ = s.batch(2)
                        project(b2, r2 % 2, b * 2 + 2)
                    if h == 2 and attends_before:
                        project_out(b - 1)
                    if h == 5:
                        if attends_before:
                            pe.wait_ge(o_lo_done, b)
                        attend(b, r, 0)
                    if h == 6 and ahead1:
                        if ahead2:
                            pe.wait_ge(q_rest_done, b2 + 1)
                        turn_maxima(b1, 0)
                    if ffn and not s.odd and h >= 4:
                        up(s.pair, s.pair_buf, h - 4)
                    if ffn and s.odd and h < 4:
                        up(s.pair, s.pair_buf, h + 4)
                    if ffn and s.odd and h >= 4:
                        for t in range(4):
                            down(s.pair, (h - 4) // 2, (h % 2) * 4 + t)

            def last():
                attend(B - 1, (B - 1) % RING, 1)
                project_out(B - 1)
                for t in range(HT):
                    up(B // 2 - 1, 1, t)
                for bi in range(2):
                    for t in range(HT):
                        down(B // 2 - 1, bi, t)

            pipeline(pe, first, slot, last)

        @block.scalar
        def _(act):
            def split_projection(b, i, r):
                act.wait_ge(projected, b + 1)
                if not (isinstance(b, int) and b < 2):
                    act.wait_ge(parts_stored, (b - 1) * 32)
                nc.scalar.copy(q_parts[i][:, 1, :], ps_proj[:, 0:T]).then_inc(q_hi_done, 1)
                nc.scalar.copy(v_ones[r][:, :, :, 0:DK],
                               ps_proj[:, T:2 * T].rearrange("p (t h d) -> p t h d", t=TT, h=NH)).then_inc(v_done, 1)

            def copy_maxima(b, half):
                act.wait_ge(max_turned, b * 2 + (half + 1))
                nc.scalar.copy(neg_max_rows[half][:, :], ps_neg_max).then_inc(max_copied, 1)

            def exps(b, h):
                act.wait_ge(exp_scored, b * NH + (h + 1))
                if h % HALF == 0 and not (isinstance(b, int) and b == 0):
                    act.wait_ge(attended, b * 2 + (h // HALF - 1))
                nc.scalar.activation(probs[:, h, :], ps_exp[h % 2][:, :], ACT.Exp, scale=SCALE).then_inc(exp_done, 1)

            def o_high(b, pair_buf, bi):
                act.wait_ge(out_projected, b + 1)
                nc.scalar.copy(o_hi[pair_buf][:, :, bi, :],
                               ps_ctx[:, 0:T].rearrange("p (t d) -> p t d", t=TT)).then_inc(o_hi_done, 1)

            def relu(pair, t):
                act.wait_ge(up_done, pair * HT + (t + 1))
                nc.scalar.activation(hidden[:, t, :], ps_up[:, 0:2 * D], ACT.Relu,
                                     scale=up_sc[:, t:t + 1]).then_inc(relu_done, 1)

            def slot(s, attends_before, ffn, ahead1, ahead2):
                b, r, _ = s.batch(0)
                for h in range(NH):
                    if h == 0:
                        copy_maxima(b, 1)
                    exps(b, h)
                    if h == 2 and ahead2:
                        b2, r2, _ = s.batch(2)
                        split_projection(b2, r2 % 2, r2)
                    if h == 3 and attends_before:
                        o_high(b - 1, ((r - 1) % RING) // 2, (r - 1) % 2)
                    if h == 6 and ahead1:
                        copy_maxima(s.batch(1)[0], 0)
                    if ffn and not s.odd and h >= 4:
                        relu(s.pair, h - 4)
                    if ffn and s.odd and h < 4:
                        relu(s.pair, h + 4)

            def last():
                o_high(B - 1, 1, 1)
                for t in range(HT):
                    relu(B // 2 - 1, t)

            def first():
                for b in range(2):
                    split_projection(b, b, b)
                copy_maxima(0, 0)
                act.wait_ge(ffn_loaded, 32)
                nc.scalar.sign(up_sign[:, :, :], up_raw[:, :, :]).then_inc(signs_made, 1)
                nc.scalar.sign(down_sign[:, :, :], down_raw[:, :, :]).then_inc(signs_made, 1)
                act.wait_ge(scales_loaded, 48)

            pipeline(act, first, slot, last)

        @block.vector
        def _(dve):
            def split_projection(b, i):
                if not (isinstance(b, int) and b == 0):
                    dve.wait_ge(q_lo_done, b)
                dve.wait_ge(v_done, b + 1)
                dve.wait_ge(q_hi_done, b + 1)
                nc.vector.tensor_tensor(q_rest[:, :], ps_proj[:, 0:T], q_parts[i][:, 1, :],
                                        ALU.subtract).then_inc(q_rest_done, 1)
                dve.wait_ge(q_rest_done, b + 1)
                nc.vector.tensor_copy(q_parts[i][:, 0, :], q_rest[:, :]).then_inc(q_mid_done, 1)
                dve.wait_ge(q_mid_done, b + 1)
                nc.vector.tensor_tensor(q_parts[i][:, 2, :], q_rest[:, :], q_parts[i][:, 0, :],
                                        ALU.subtract).then_inc(q_lo_done, 1)

            def maximum(b, h):
                dve.wait_ge(max_scored, b * NH + (h + 1))
                nc.vector.reduce_max(maxima[:, h // HALF, h % HALF, :],
                                     ps_max[h % 2][:, :].rearrange("p (t k) -> p t k", t=TT),
                                     AX_X).then_inc(maxed, 1)

            def split_maxima(b, half):
                m = maxima[:, half, :, :].rearrange("p h t -> p (h t)")
                dve.wait_ge(maxed, b * NH + (half + 1) * HALF)
                nc.vector.tensor_scalar(neg_max[:, half, 0, :], m, -1.0, None, ALU.mult).then_inc(max_hi_done, 1)
                dve.wait_ge(max_hi_done, b * 2 + (half + 1))
                nc.vector.scalar_tensor_tensor(out=neg_max[:, half, 1, :], in0=m, scalar=-1.0,
                                               in1=neg_max[:, half, 0, :], op0=ALU.mult,
                                               op1=ALU.subtract).then_inc(max_split, 1)

            def normalise(b):
                turned = turned_context[:, :].rearrange("p (n c) -> p n c", c=32)
                dve.wait_ge(attended, b * 2 + 2)
                nc.vector.transpose(turned_context[:, :], ps_ctx[:, :]).then_inc(context_turned, 1)
                dve.wait_ge(context_turned, b + 1)
                nc.vector.reciprocal(inverse_sums[:, :], turned[:, :, DK]).then_inc(inverted, 1)
                dve.wait_ge(inverted, b + 1)
                if not (isinstance(b, int) and b == 0):
                    dve.wait_ge(context_done, b)
                nc.vector.tensor_tensor(normal_context[:, :].rearrange("p (n c) -> p n c", c=32)[:, :, 0:DK],
                                        turned[:, :, 0:DK],
                                        inverse_sums[:, :].rearrange("p (n a) -> p n a", a=1).broadcast_to(
                                            [P, BLOCKS, DK]), ALU.mult).then_inc(normalised, 1)
                dve.wait_ge(normalised, b + 1)
                nc.vector.transpose(context[:, :, :].rearrange("p g t -> p (g t)"),
                                    normal_context[:, :]).then_inc(context_done, 1)

            def o_low(b, pair_buf, bi):
                dve.wait_ge(o_hi_done, b + 1)
                nc.vector.tensor_tensor(o_lo[pair_buf][:, :, bi, :],
                                        ps_ctx[:, 0:T].rearrange("p (t d) -> p t d", t=TT),
                                        o_hi[pair_buf][:, :, bi, :], ALU.subtract).then_inc(o_lo_done, 1)

            def hid_high(pair, t):
                dve.wait_ge(relu_done, pair * HT + (t + 1))
                nc.vector.tensor_copy(hid_hi[:, t, :], hidden[:, t, :]).then_inc(hid_hi_done, 1)

            def scale_out(pair):
                dve.wait_ge(down_done, pair + 1)
                nc.vector.tensor_tensor(out_all[:, bass.ds(pair * 2, 2), :],
                                        ps_down[:, :].rearrange("p (b t) -> p b t", b=2),
                                        out_scale[:, :].rearrange("p (a t) -> p a t", a=1).broadcast_to([P, 2, T]),
                                        ALU.mult).then_inc(scaled, 1)

            def first():
                dve.wait_ge(mask_loaded, 16)
                nc.vector.tensor_copy(r16[:, :], mask16[:, :])
                nc.vector.tensor_scalar(neg16[:, :], mask16[:, :], -NEG, NEG, ALU.mult,
                                        ALU.add).then_inc(mask_rows_made, 1)
                for r in range(RING):
                    one = nc.vector.memset(key_stack[r][6 * DK:K_ALL, :, :], 1.0)
                for i in range(RING):
                    one = nc.vector.memset(v_ones[i][:, :, :, DK:2 * DK], 1.0)
                nc.vector.memset(normal_context[:, :], 0.0)
                one.then_inc(constants_set, 1)
                for b in range(2):
                    split_projection(b, b)
                for h in range(NH):
                    maximum(0, h)
                    if h == HALF - 1:
                        split_maxima(0, 0)
                split_maxima(0, 1)
                dve.wait_ge(scales_loaded, 48)
                nc.vector.tensor_scalar(out_scale[:, :], down_sc[:, :], out_sc[:, 0:1], None,
                                        ALU.mult).then_inc(scale_made, 1)
                dve.wait_ge(scale_made, 1)

            def slot(s, attends_before, ffn, ahead1, ahead2):
                b, r, _ = s.batch(0)
                for h in range(NH):
                    if ahead1:
                        b1 = s.batch(1)[0]
                        maximum(b1, h)
                        if h == HALF - 1:
                            split_maxima(b1, 0)
                        if h == NH - 1:
                            split_maxima(b1, 1)
                    if h == 1 and attends_before:
                        normalise(b - 1)
                    if h == 2 and ahead2:
                        b2, r2, _ = s.batch(2)
                        split_projection(b2, r2 % 2)
                    if h == 3 and attends_before:
                        o_low(b - 1, ((r - 1) % RING) // 2, (r - 1) % 2)
                    if ffn and not s.odd and h >= 4:
                        hid_high(s.pair, h - 4)
                    if ffn and s.odd and h < 4:
                        hid_high(s.pair, h + 4)
                if ffn and s.odd:
                    scale_out(s.pair)

            def last():
                normalise(B - 1)
                o_low(B - 1, 1, 1)
                for t in range(HT):
                    hid_high(B // 2 - 1, t)
                scale_out(B // 2 - 1)

            pipeline(dve, first, slot, last)


def kernel(x, cond_2048, L0_cond_Wq, L0_cond_Wo, L0_ffn_up_weight, L0_ffn_down_weight, L0_ffn_up_scale,
           L0_ffn_down_scale, L0_ffn_output_scale):
    import numpy as np
    import concourse.bacc as bacc
    from concourse import mybir as mb
    from concourse.bass_utils import run_bass_kernel_spmd

    nc = bacc.Bacc("TRN2", target_bir_lowering=False, num_devices=1)
    wq_t = np.asarray(L0_cond_Wq).T
    laid = {
        "x": np.asarray(x),
        "mask": np.asarray(cond_2048),
        "wq_by_head": wq_t,
        "wq_by_dim": wq_t.reshape(D, NH, DK).transpose(0, 2, 1).reshape(D, D),
        "wo_t": np.asarray(L0_cond_Wo).T,
        "up_t": np.asarray(L0_ffn_up_weight).T,
        "down_t": np.asarray(L0_ffn_down_weight).T,
        "up_scale": np.asarray(L0_ffn_up_scale).reshape(HT, P).T,
        "down_scale": np.asarray(L0_ffn_down_scale),
        "output_scale": np.asarray(L0_ffn_output_scale),
    }
    laid = {f"in_{k}": np.ascontiguousarray(v) for k, v in laid.items()}
    args = [nc.dram_tensor(k, v.shape, mb.dt.from_np(v.dtype), kind="ExternalInput").ap() for k, v in laid.items()]
    out = nc.dram_tensor("out", (B, D, T), F32, kind="ExternalOutput").ap()
    attention_ffn(nc, *args, out)
    r = run_bass_kernel_spmd(nc, [laid], core_ids=[0])
    return r.results[0]["out"]
```

```python
from contextlib import ExitStack

import concourse.bass as bass
from concourse import mybir

F32 = mybir.dt.float32
F32R = mybir.dt.float32r
BF16 = mybir.dt.bfloat16
ACT = mybir.ActivationFunctionType
ALU = mybir.AluOpType
AX_X = mybir.AxisListType.X

B, D, T = 16, 128, 256
NH = 8
DK = D // NH
HID = 1024
P = 128
UP_FROM = 5
TT = T // P
HT = HID // P
HALF = NH // 2
SCALE = DK ** -0.5
NEG = -1e30 / SCALE
BLOCKS = 2 * T // 32
RING = 4

ROW_MID, ROW_HI, ROW_R, ROW_LO, ROW_NEG = 0, DK, 2 * DK, 2 * DK + 1, 3 * DK + 1
ROWS = 3 * DK + 2
K_MASKED = 6 * DK + 1
K_ALL = K_MASKED + 2


class Slot:

    def __init__(self, turn, j):
        self.turn, self.j = turn, j
        self.b = turn * RING + (2 + j)
        self.odd = j % 2 == 1
        self.pair = turn * 2 + j // 2
        self.pair_buf = (j // 2) % 2

    def batch(self, d):
        n = 2 + self.j + d
        return self.turn * RING + n, n % RING, self.turn + n // RING


def attention_ffn(nc, x, mask, wq_by_head, wq_by_dim, wo_t, up_t, down_t, up_scale, down_scale,
                  output_scale, out):
    parts = nc.dram_tensor("parts_dram", (B + 1, ROWS, NH * T), BF16, kind="Internal").ap()
    ctx = ExitStack()
    with ctx:
        def sb(name, shape, dt=F32):
            return ctx.enter_context(nc.sbuf_tensor(name, shape, dt))

        def pb(name):
            return ctx.enter_context(nc.psum_tensor(name, [P, 512], F32))

        def sem(name):
            return ctx.enter_context(nc.semaphore(name))

        x_all = sb("x_all", [P, B + 1, T])
        mask_all = sb("mask_all", [P, B + 1, T])
        out_all = sb("out_all", [P, B, T])
        wq_h = sb("wq_h", [P, D])
        wq_d = sb("wq_d", [P, D])
        wo_pad = sb("wo_pad", [P, 2, D])
        up_raw = sb("up_raw", [P, TT, HID])
        down_raw = sb("down_raw", [P, HT, T])
        up_sign = sb("up_sign", [P, TT, HID], F32R)
        down_sign = sb("down_sign", [P, HT, T], F32R)
        up_sc = sb("up_sc", [P, HT])
        down_sc = sb("down_sc", [P, T])
        out_sc = sb("out_sc", [P, 1])
        out_scale = sb("out_scale", [P, T])
        ident = sb("ident", [P, P], BF16)
        mask16 = sb("mask16", [B, T])
        r16 = sb("r16", [B, T], BF16)
        neg16 = sb("neg16", [B, T], BF16)
        x_masked = [sb(f"x_masked{i}", [P, T]) for i in range(2)]
        x_copy = [sb(f"x_copy{i}", [P, T]) for i in range(2)]
        q_parts = [sb(f"q_parts{i}", [P, 3, T], BF16) for i in range(2)]
        q_rest = sb("q_rest", [P, T])
        key_stack = [sb(f"key_stack{i}", [P, NH, T], BF16) for i in range(RING)]
        query_stack = [sb(f"query_stack{i}", [P, NH, T], BF16) for i in range(RING)]
        v_ones = [sb(f"v_ones{i}", [P, TT, NH, 32]) for i in range(RING)]
        maxima = sb("maxima", [P, 2, HALF, TT])
        neg_max = sb("neg_max", [P, 2, 2, HALF * TT], BF16)
        neg_max_rows = [sb(f"neg_max_rows{i}", [2 * HALF * TT, P], BF16) for i in range(2)]
        probs = sb("probs", [P, NH, TT * T])
        turned_context = sb("turned_context", [P, 2 * T])
        inverse_sums = sb("inverse_sums", [P, BLOCKS])
        normal_context = sb("normal_context", [P, 2 * T])
        context = sb("context", [P, 2, T])
        o_hi = [sb(f"o_hi{i}", [P, TT, 2, D], F32R) for i in range(2)]
        o_lo = [sb(f"o_lo{i}", [P, TT, 2, D], F32R) for i in range(2)]
        hidden = sb("hidden", [P, HT, 2 * D])
        hid_hi = sb("hid_hi", [P, HT, 2 * D], F32R)
        hid_lo = sb("hid_lo", [P, HT, 2 * D], F32R)

        ps_exp = [pb(f"ps_exp{i}") for i in range(2)]
        ps_max = [pb(f"ps_max{i}") for i in range(2)]
        ps_ctx = pb("ps_ctx")
        ps_proj = pb("ps_proj")
        ps_up = pb("ps_up")
        ps_down = pb("ps_down")
        ps_neg_max = ps_proj[0:2 * HALF * TT, 0:P // 2].bitcast(BF16)

        weights_loaded, wo_loaded = sem("weights_loaded"), sem("wo_loaded")
        x_first, x_rest = sem("x_first"), sem("x_rest")
        mask_loaded, mask_stored = sem("mask_loaded"), sem("mask_stored")
        ffn_loaded, scales_loaded = sem("ffn_loaded"), sem("scales_loaded")
        parts_stored = sem("parts_stored")
        stack_loaded = [sem(f"stack_loaded{i}") for i in range(RING)]
        max_loaded = [sem(f"max_loaded{i}") for i in range(2)]
        out_stored = sem("out_stored")
        zeroed, constants_set = sem("zeroed"), sem("constants_set")
        ident_zeroed, ident_made = sem("ident_zeroed"), sem("ident_made")
        x_masked_ready, x_copied = sem("x_masked_ready"), sem("x_copied")
        hid_lo_done, out_ready = sem("hid_lo_done"), sem("out_ready")
        q_projected, v_projected = sem("q_projected"), sem("v_projected")
        max_scored, exp_scored = sem("max_scored"), sem("exp_scored")
        max_turned, attended, out_projected = sem("max_turned"), sem("attended"), sem("out_projected")
        up_done, down_done = sem("up_done"), sem("down_done")
        signs_made = sem("signs_made")
        q_hi_done, v_done, max_copied = sem("q_hi_done"), sem("v_done"), sem("max_copied")
        exp_done, o_hi_done, relu_done = sem("exp_done"), sem("o_hi_done"), sem("relu_done")
        mask_rows_made = sem("mask_rows_made")
        scale_made = sem("scale_made")
        q_rest_done, q_mid_done, q_lo_done = sem("q_rest_done"), sem("q_mid_done"), sem("q_lo_done")
        maxed, max_hi_done, max_split = sem("maxed"), sem("max_hi_done"), sem("max_split")
        context_turned, inverted, normalised = sem("context_turned"), sem("inverted"), sem("normalised")
        context_done, o_lo_done = sem("context_done"), sem("o_lo_done")
        hid_hi_done, scaled = sem("hid_hi_done"), sem("scaled")

        block = ctx.enter_context(nc.Block())

        def pipeline(engine, first, slot, last):
            first()
            for j in (-2, -1):
                slot(Slot(0, j), before=j == -1, ffn=False, ahead1=True, ahead2=True, ahead3=True)
            with engine.Fori(0, (B - RING) // RING) as turn:
                for j in range(RING):
                    slot(Slot(turn, j), before=True, ffn=True, ahead1=True, ahead2=True, ahead3=True)
            for j in (0, 1):
                slot(Slot((B - RING) // RING, j), before=True, ffn=True, ahead1=j == 0, ahead2=False, ahead3=False)
            last()

        @block.sync
        def _(sp):
            def load_parts(b, r):
                def rows(at, n, twice=False):
                    src = parts[b, at:at + n, :]
                    if twice:
                        src = bass.AP(src.tensor, src.offset, [[0, 2], [NH * T, n], [1, NH * T]])
                    return src
                key, query, done = key_stack[r], query_stack[r], stack_loaded[r]
                sp.dma_start(key[0:2 * DK, :, :], rows(ROW_MID, DK, True)).then_inc(done, 16)
                sp.dma_start(query[0:4 * DK, :, :], rows(ROW_MID, 2 * DK, True)).then_inc(done, 16)
                sp.dma_start(key[2 * DK:4 * DK, :, :], rows(ROW_HI, DK, True)).then_inc(done, 16)
                sp.dma_start(key[4 * DK:5 * DK, :, :], rows(ROW_HI, DK)).then_inc(done, 16)
                sp.dma_start(query[4 * DK:5 * DK, :, :], rows(ROW_LO, DK)).then_inc(done, 16)
                sp.dma_start(key[5 * DK:K_MASKED, :, :], rows(ROW_LO, DK + 1)).then_inc(done, 16)
                sp.dma_start(query[5 * DK:K_MASKED, :, :], rows(ROW_HI, DK + 1)).then_inc(done, 16)

            def store_parts(b, i):
                dst = parts[b, 0:2 * DK, :].rearrange("(s d) (h t) -> (d h) s t", s=2, h=NH)
                sp.wait_ge(q_hi_done, b + 1)
                sp.wait_ge(q_mid_done, b + 1)
                sp.dma_start(dst, q_parts[i][:, 0:2, :]).then_inc(parts_stored, 16)
                dst = parts[b, ROW_LO:ROW_LO + DK, :].rearrange("d (h t) -> (d h) t", h=NH)
                sp.wait_ge(q_lo_done, b + 1)
                sp.dma_start(dst, q_parts[i][:, 2, :]).then_inc(parts_stored, 16)

            def first():
                sp.dma_start(x_all[:, 0:2, :], x[0:2].rearrange("b p t -> p b t")).then_inc(x_first, 16)
                sp.dma_start(mask_all[:, 0:2, :], mask[0:2, :].partition_broadcast(P)).then_inc(x_first, 16)
                sp.dma_start(wq_d[:, :], wq_by_dim).then_inc(weights_loaded, 16)
                sp.dma_start(mask16[:, :], mask).then_inc(mask_loaded, 16)
                sp.dma_start(wq_h[:, :], wq_by_head).then_inc(weights_loaded, 16)
                sp.wait_ge(mask_rows_made, 1)
                for row, rows in ((ROW_R, r16), (ROW_NEG, neg16)):
                    src = rows[:, :].rearrange("b (a t) -> b a t", a=1).broadcast_to([B, NH, T])
                    sp.dma_start(parts[0:B, row, :].rearrange("b (h t) -> b h t", h=NH), src).then_inc(mask_stored, 16)
                store_parts(0, 0)
                sp.dma_start(x_all[:, 2:B, :], x[2:B].rearrange("b p t -> p b t")).then_inc(x_rest, 16)
                sp.wait_ge(mask_stored, 2 * 16)
                sp.wait_ge(constants_set, 1)
                sp.wait_ge(parts_stored, 32)
                load_parts(0, 0)
                store_parts(1, 1)
                sp.dma_start(mask_all[:, 2:B, :], mask[2:B, :].partition_broadcast(P)).then_inc(x_rest, 16)
                sp.dma_start(x_all[:, B, :], x[0]).then_inc(x_rest, 16)
                sp.dma_start(mask_all[:, B, :], mask[0, :].partition_broadcast(P)).then_inc(x_rest, 16)
                sp.wait_ge(parts_stored, 64)
                sp.wait_ge(constants_set, 2)
                load_parts(1, 1)
                store_parts(2, 0)
                load_maxima(0, 0, 0)
                sp.wait_ge(zeroed, 1)
                for j in range(HALF):
                    sp.dma_start(wo_pad[32 * j:32 * j + DK, :, :],
                                 wo_t.rearrange("(g j d) o -> j d g o", g=2, j=HALF)[j]).then_inc(wo_loaded, 16)
                sp.dma_start(up_raw[:, :, :], up_t.rearrange("(k p) n -> p k n", p=P)).then_inc(ffn_loaded, 16)
                sp.dma_start(down_raw[:, :, :], down_t.rearrange("(k p) n -> p k n", p=P)).then_inc(ffn_loaded, 16)
                sp.dma_start(up_sc[:, :], up_scale).then_inc(scales_loaded, 16)
                sp.dma_start(down_sc[:, :], down_scale.partition_broadcast(P)).then_inc(scales_loaded, 16)
                sp.dma_start(out_sc[:, :], output_scale.partition_broadcast(P)).then_inc(scales_loaded, 16)
                sp.wait_ge(constants_set, RING)

            def load_maxima(b, r, half):
                sp.wait_ge(max_copied, b * 2 + (half + 1))
                sp.dma_start(query_stack[r][K_MASKED:K_ALL, half * HALF:(half + 1) * HALF, :],
                             neg_max_rows[half][:, :]).then_inc(max_loaded[half], 16)

            def store_out(pair):
                sp.wait_ge(out_ready, pair + 1)
                sp.dma_start(out[bass.ds(pair * 2, 2)].rearrange("b p t -> p b t"),
                             out_all[:, bass.ds(pair * 2, 2), :]).then_inc(out_stored, 16)

            def slot(s, before, ffn, ahead1, ahead2, ahead3):
                b, r, _ = s.batch(0)
                load_maxima(b, r, 1)
                if ahead2:
                    b2, r2, _ = s.batch(2)
                    sp.wait_ge(parts_stored, b2 * 32 + 32)
                    load_parts(b2, r2)
                if ahead3:
                    b3, r3, _ = s.batch(3)
                    store_parts(b3, r3 % 2)
                if ahead1:
                    b1, r1, _ = s.batch(1)
                    load_maxima(b1, r1, 0)
                if ffn and s.odd:
                    store_out(s.pair)

            def last():
                store_out(B // 2 - 1)
                sp.wait_ge(out_stored, 16 * (B // 2))

            pipeline(sp, first, slot, last)

        @block.gpsimd
        def _(pool):
            def mask_x(b, i):
                nc.gpsimd.tensor_tensor(x_masked[i][:, :], x_all[:, b, :], mask_all[:, b, :],
                                        ALU.mult).then_inc(x_masked_ready, 1)

            def copy_x(b, i):
                nc.gpsimd.tensor_copy(x_copy[i][:, :], x_all[:, b, :]).then_inc(x_copied, 1)

            def first():
                pool.wait_ge(x_first, 32)
                mask_x(0, 0)
                mask_x(1, 1)
                copy_x(0, 0)
                copy_x(1, 1)
                nc.gpsimd.memset(ident[:, :], 0.0).then_inc(ident_zeroed, 1)
                pool.wait_ge(ident_zeroed, 1)
                nc.gpsimd.affine_select(out=ident[:, :], in_=ident[:, :], compare_op=ALU.not_equal, fill=1.0,
                                        base=0, pattern=[[-1, P]], channel_multiplier=1).then_inc(ident_made, 1)
                nc.gpsimd.memset(wo_pad[:, :, :], 0.0).then_inc(zeroed, 1)
                pool.wait_ge(x_rest, 64)
                pool.wait_ge(q_projected, 1)
                mask_x(2, 0)

            def hid_low(pair, t):
                pool.wait_ge(hid_hi_done, pair * HT + (t + 1))
                nc.gpsimd.tensor_tensor(hid_lo[:, t, :], hidden[:, t, :], hid_hi[:, t, :],
                                        ALU.subtract).then_inc(hid_lo_done, 1)

            def residual(pair):
                pool.wait_ge(scaled, pair + 1)
                o = out_all[:, bass.ds(pair * 2, 2), :]
                nc.gpsimd.tensor_tensor(o, o, x_all[:, bass.ds(pair * 2, 2), :], ALU.add).then_inc(out_ready, 1)

            def slot(s, before, ffn, ahead1, ahead2, ahead3):
                if ahead3:
                    b2, r2, _ = s.batch(2)
                    b3, r3, _ = s.batch(3)
                    pool.wait_ge(v_projected, b2 - 1)
                    pool.wait_ge(q_projected, b3 - 1)
                    mask_x(b3, r3 % 2)
                    copy_x(b2, r2 % 2)
                if ffn:
                    first_t = NH - UP_FROM - 1
                    for t in range(first_t, HT) if s.odd else range(first_t):
                        hid_low(s.pair, t)
                    if s.odd:
                        residual(s.pair)

            def last():
                for t in range(HT):
                    hid_low(B // 2 - 1, t)
                residual(B // 2 - 1)

            pipeline(pool, first, slot, last)

        @block.tensor
        def _(pe):
            def project_q(b, i, copied):
                pe.wait_ge(x_masked_ready, b + 1)
                if copied is not None:
                    pe.wait_ge(max_copied, copied)
                nc.tensor.matmul(ps_proj[:, 0:T], wq_d[:, :], x_masked[i][:, :],
                                 start=True, stop=True).then_inc(q_projected, 1)

            def project_v(b, i):
                pe.wait_ge(x_copied, b + 1)
                if not (isinstance(b, int) and b == 0):
                    pe.wait_ge(v_done, b)
                for t in range(TT):
                    mm = nc.tensor.matmul(ps_down[:, t * D:(t + 1) * D], x_copy[i][:, t * P:(t + 1) * P],
                                          wq_h[:, :], start=True, stop=True)
                mm.then_inc(v_projected, 1)

            def score_max(b, r, uses, h):
                if h == 0:
                    pe.wait_ge(stack_loaded[r], uses * 112 + 112)
                if not (isinstance(b, int) and b == 0 and h < 2):
                    pe.wait_ge(maxed, b * NH + (h - 1))
                for t in range(TT):
                    mm = nc.tensor.matmul(ps_max[h % 2][:, t * T:(t + 1) * T],
                                          query_stack[r][0:K_MASKED, h, t * P:(t + 1) * P],
                                          key_stack[r][0:K_MASKED, h, :], start=True, stop=True)
                mm.then_inc(max_scored, 1)

            def score_exp(b, r, h):
                if h % HALF == 0:
                    pe.wait_ge(max_loaded[h // HALF], b * 16 + 16)
                if not (isinstance(b, int) and b == 0 and h < 2):
                    pe.wait_ge(exp_done, b * NH + (h - 1))
                for t in range(TT):
                    mm = nc.tensor.matmul(ps_exp[h % 2][:, t * T:(t + 1) * T],
                                          key_stack[r][0:K_ALL, h, t * P:(t + 1) * P],
                                          query_stack[r][0:K_ALL, h, :], start=True, stop=True)
                mm.then_inc(exp_scored, 1)

            def turn_maxima(b, half):
                pe.wait_ge(max_split, b * 2 + (half + 1))
                if half == 1:
                    pe.wait_ge(max_copied, b * 2 + 1)
                nc.tensor.transpose(ps_neg_max, neg_max[:, half, :, :].rearrange("p s c -> p (s c)"),
                                    ident[:, :]).then_inc(max_turned, 1)

            def attend(b, r, half):
                pe.wait_ge(exp_done, b * NH + (half + 1) * HALF)
                if half == 0:
                    pe.wait_ge(v_done, b + 1)
                for t in range(TT):
                    for j in range(HALF):
                        h = half * HALF + j
                        mm = nc.tensor.matmul(ps_ctx[32 * j:32 * j + 32, half * T:(half + 1) * T],
                                              v_ones[r][:, t, h, :], probs[:, h, t * T:(t + 1) * T],
                                              start=t == 0, stop=t == TT - 1)
                mm.then_inc(attended, 1)

            def project_out(b):
                pe.wait_ge(context_done, b + 1)
                for t in range(TT):
                    for g in range(2):
                        mm = nc.tensor.matmul(ps_ctx[:, t * D:(t + 1) * D], context[:, g, t * P:(t + 1) * P],
                                              wo_pad[:, g, :], start=g == 0, stop=g == 1)
                mm.then_inc(out_projected, 1)

            def up(pair, i, t):
                if t == 0:
                    pe.wait_ge(o_lo_done, pair * 2 + 2)
                else:
                    pe.wait_ge(relu_done, pair * HT + t)
                for n, (k, part) in enumerate((k, part) for k in range(TT) for part in (o_hi, o_lo)):
                    mm = nc.tensor.matmul(ps_up[:, 0:2 * D], up_sign[:, k, t * P:(t + 1) * P],
                                          part[i][:, k, :, :].rearrange("p b s -> p (b s)"),
                                          start=n == 0, stop=n == 2 * TT - 1)
                mm.then_inc(up_done, 1)

            def down(pair, bi, t):
                if bi == 0:
                    pe.wait_ge(hid_lo_done, pair * HT + (t + 1))
                for part in (hid_hi, hid_lo):
                    mm = nc.tensor.matmul(ps_down[:, bi * T:(bi + 1) * T], part[:, t, bi * D:(bi + 1) * D],
                                          down_sign[:, t, :], start=t == 0 and part is hid_hi,
                                          stop=t == HT - 1 and part is hid_lo)
                if bi == 1 and t == HT - 1:
                    mm.then_inc(down_done, 1)

            def first():
                pe.wait_ge(weights_loaded, 32)
                project_q(0, 0, None)
                pe.wait_ge(q_rest_done, 1)
                project_q(1, 1, None)
                project_v(0, 0)
                project_v(1, 1)
                pe.wait_ge(q_rest_done, 2)
                project_q(2, 0, None)
                pe.wait_ge(ident_made, 1)
                for h in range(NH):
                    score_max(0, 0, 0, h)
                    if h == 5:
                        pe.wait_ge(q_rest_done, 3)
                        turn_maxima(0, 0)

            def slot(s, before, ffn, ahead1, ahead2, ahead3):
                b, r, uses = s.batch(0)
                if ahead1:
                    b1, r1, uses1 = s.batch(1)
                if ahead2:
                    b2, r2, _ = s.batch(2)
                    b3, r3, _ = s.batch(3)
                for h in range(NH):
                    score_exp(b, r, h)
                    if ahead1:
                        score_max(b1, r1, uses1, h)
                    if h == 0:
                        turn_maxima(b, 1)
                    if h == 0 and before:
                        attend(b - 1, (r - 1) % RING, 1)
                    if h == 2 and ahead3:
                        project_q(b3, r3 % 2, b * 2 + 2)
                    if h == 3 and before:
                        if isinstance(b, int) and b == 1:
                            pe.wait_ge(wo_loaded, 16 * HALF)
                        project_out(b - 1)
                    if h == 3 and ahead2:
                        project_v(b2, r2 % 2)
                    if h == 4 and ahead1:
                        if ahead3:
                            pe.wait_ge(q_rest_done, b3 + 1)
                        turn_maxima(b1, 0)
                    if h == 5:
                        if before:
                            pe.wait_ge(o_lo_done, b)
                        attend(b, r, 0)
                    if ffn and not s.odd and h >= UP_FROM:
                        up(s.pair, s.pair_buf, h - UP_FROM)
                    if ffn and s.odd and h < UP_FROM:
                        up(s.pair, s.pair_buf, h + NH - UP_FROM)
                    if ffn and s.odd and h >= UP_FROM:
                        if h == UP_FROM and ahead2:
                            pe.wait_ge(v_done, b2 + 1)
                        n = 2 * HT // (NH - UP_FROM)
                        for i in range((h - UP_FROM) * n, (h - UP_FROM + 1) * n if h < NH - 1 else 2 * HT):
                            down(s.pair, i // HT, i % HT)
                if isinstance(b, int) and b == 1:
                    pe.wait_ge(signs_made, 2)

            def last():
                attend(B - 1, (B - 1) % RING, 1)
                project_out(B - 1)
                for t in range(HT):
                    up(B // 2 - 1, 1, t)
                for bi in range(2):
                    for t in range(HT):
                        down(B // 2 - 1, bi, t)

            pipeline(pe, first, slot, last)

        @block.scalar
        def _(act):
            def q_high(b, i):
                act.wait_ge(q_projected, b + 1)
                if not (isinstance(b, int) and b < 2):
                    act.wait_ge(parts_stored, (b - 1) * 32)
                nc.scalar.copy(q_parts[i][:, 1, :], ps_proj[:, 0:T]).then_inc(q_hi_done, 1)

            def values(b, r):
                act.wait_ge(v_projected, b + 1)
                nc.scalar.copy(v_ones[r][:, :, :, 0:DK],
                               ps_down[:, 0:T].rearrange("p (t h d) -> p t h d", t=TT, h=NH)).then_inc(v_done, 1)

            def copy_maxima(b, half):
                act.wait_ge(max_turned, b * 2 + (half + 1))
                nc.scalar.copy(neg_max_rows[half][:, :], ps_neg_max).then_inc(max_copied, 1)

            def exps(b, h):
                act.wait_ge(exp_scored, b * NH + (h + 1))
                if h % HALF == 0 and not (isinstance(b, int) and b == 0):
                    act.wait_ge(attended, b * 2 + (h // HALF - 1))
                nc.scalar.activation(probs[:, h, :], ps_exp[h % 2][:, :], ACT.Exp, scale=SCALE).then_inc(exp_done, 1)

            def o_high(b, pair_buf, bi):
                act.wait_ge(out_projected, b + 1)
                nc.scalar.copy(o_hi[pair_buf][:, :, bi, :],
                               ps_ctx[:, 0:T].rearrange("p (t d) -> p t d", t=TT)).then_inc(o_hi_done, 1)

            def relu(pair, t):
                act.wait_ge(up_done, pair * HT + (t + 1))
                nc.scalar.activation(hidden[:, t, :], ps_up[:, 0:2 * D], ACT.Relu,
                                     scale=up_sc[:, t:t + 1]).then_inc(relu_done, 1)

            def slot(s, before, ffn, ahead1, ahead2, ahead3):
                b, r, _ = s.batch(0)
                for h in range(NH):
                    exps(b, h)
                    if h == 0:
                        copy_maxima(b, 1)
                    if h == 2 and ahead3:
                        b3, r3, _ = s.batch(3)
                        q_high(b3, r3 % 2)
                    if h == 3 and before:
                        o_high(b - 1, ((r - 1) % RING) // 2, (r - 1) % 2)
                    if h == 3 and ahead2:
                        b2, r2, _ = s.batch(2)
                        values(b2, r2)
                    if h == 4 and ahead1:
                        copy_maxima(s.batch(1)[0], 0)
                    if ffn and not s.odd and h >= UP_FROM:
                        relu(s.pair, h - UP_FROM)
                    if ffn and s.odd and h < UP_FROM:
                        relu(s.pair, h + NH - UP_FROM)
                    if isinstance(b, int) and b == 0 and h == 4:
                        act.wait_ge(ffn_loaded, 32)
                        nc.scalar.sign(up_sign[:, :, :], up_raw[:, :, :]).then_inc(signs_made, 1)
                    if isinstance(b, int) and b == 1 and h == 4:
                        nc.scalar.sign(down_sign[:, :, :], down_raw[:, :, :]).then_inc(signs_made, 1)
                        act.wait_ge(scales_loaded, 48)

            def last():
                o_high(B - 1, 1, 1)
                for t in range(HT):
                    relu(B // 2 - 1, t)

            def first():
                q_high(0, 0)
                q_high(1, 1)
                values(0, 0)
                values(1, 1)
                q_high(2, 0)
                copy_maxima(0, 0)

            pipeline(act, first, slot, last)

        @block.vector
        def _(dve):
            def split_projection(b, i, steps=(0, 1, 2)):
                if 0 in steps:
                    if not (isinstance(b, int) and b == 0):
                        dve.wait_ge(q_lo_done, b)
                    dve.wait_ge(q_hi_done, b + 1)
                    nc.vector.tensor_tensor(q_rest[:, :], ps_proj[:, 0:T], q_parts[i][:, 1, :],
                                            ALU.subtract).then_inc(q_rest_done, 1)
                if 1 in steps:
                    dve.wait_ge(q_rest_done, b + 1)
                    nc.vector.tensor_copy(q_parts[i][:, 0, :], q_rest[:, :]).then_inc(q_mid_done, 1)
                if 2 in steps:
                    dve.wait_ge(q_mid_done, b + 1)
                    nc.vector.tensor_tensor(q_parts[i][:, 2, :], q_rest[:, :], q_parts[i][:, 0, :],
                                            ALU.subtract).then_inc(q_lo_done, 1)

            def maximum(b, h):
                dve.wait_ge(max_scored, b * NH + (h + 1))
                nc.vector.reduce_max(maxima[:, h // HALF, h % HALF, :],
                                     ps_max[h % 2][:, :].rearrange("p (t k) -> p t k", t=TT),
                                     AX_X).then_inc(maxed, 1)

            def split_maxima(b, half, part):
                m = maxima[:, half, :, :].rearrange("p h t -> p (h t)")
                if part == 0:
                    dve.wait_ge(maxed, b * NH + (half + 1) * HALF)
                    nc.vector.tensor_scalar(neg_max[:, half, 0, :], m, -1.0, None, ALU.mult).then_inc(max_hi_done, 1)
                else:
                    dve.wait_ge(max_hi_done, b * 2 + (half + 1))
                    nc.vector.scalar_tensor_tensor(out=neg_max[:, half, 1, :], in0=m, scalar=-1.0,
                                                   in1=neg_max[:, half, 0, :], op0=ALU.mult,
                                                   op1=ALU.subtract).then_inc(max_split, 1)

            def normalise(b, step):
                turned = turned_context[:, :].rearrange("p (n c) -> p n c", c=32)
                if step == 0:
                    dve.wait_ge(attended, b * 2 + 2)
                    nc.vector.transpose(turned_context[:, :], ps_ctx[:, :]).then_inc(context_turned, 1)
                if step == 1:
                    dve.wait_ge(context_turned, b + 1)
                    nc.vector.reciprocal(inverse_sums[:, :], turned[:, :, DK]).then_inc(inverted, 1)
                if step == 2:
                    dve.wait_ge(inverted, b + 1)
                    if not (isinstance(b, int) and b == 0):
                        dve.wait_ge(context_done, b)
                    nc.vector.tensor_tensor(normal_context[:, :].rearrange("p (n c) -> p n c", c=32)[:, :, 0:DK],
                                            turned[:, :, 0:DK],
                                            inverse_sums[:, :].rearrange("p (n a) -> p n a", a=1).broadcast_to(
                                                [P, BLOCKS, DK]), ALU.mult).then_inc(normalised, 1)
                if step == 3:
                    dve.wait_ge(normalised, b + 1)
                    nc.vector.transpose(context[:, :, :].rearrange("p g t -> p (g t)"),
                                        normal_context[:, :]).then_inc(context_done, 1)

            def o_low(b, pair_buf, bi):
                dve.wait_ge(o_hi_done, b + 1)
                nc.vector.tensor_tensor(o_lo[pair_buf][:, :, bi, :],
                                        ps_ctx[:, 0:T].rearrange("p (t d) -> p t d", t=TT),
                                        o_hi[pair_buf][:, :, bi, :], ALU.subtract).then_inc(o_lo_done, 1)

            def hid_high(pair, t):
                dve.wait_ge(relu_done, pair * HT + (t + 1))
                nc.vector.tensor_copy(hid_hi[:, t, :], hidden[:, t, :]).then_inc(hid_hi_done, 1)

            def scale_out(pair):
                dve.wait_ge(down_done, pair + 1)
                nc.vector.tensor_tensor(out_all[:, bass.ds(pair * 2, 2), :],
                                        ps_down[:, :].rearrange("p (b t) -> p b t", b=2),
                                        out_scale[:, :].rearrange("p (a t) -> p a t", a=1).broadcast_to([P, 2, T]),
                                        ALU.mult).then_inc(scaled, 1)

            def first():
                dve.wait_ge(mask_loaded, 16)
                nc.vector.tensor_copy(r16[:, :], mask16[:, :])
                nc.vector.tensor_scalar(neg16[:, :], mask16[:, :], -NEG, NEG, ALU.mult,
                                        ALU.add).then_inc(mask_rows_made, 1)
                for r in range(RING):
                    nc.vector.memset(key_stack[r][6 * DK:K_ALL, :, :], 1.0).then_inc(constants_set, 1)
                    if r == 0:
                        split_projection(0, 0)
                        split_projection(1, 1)
                    if r == 1:
                        for v in v_ones:
                            nc.vector.memset(v[:, :, :, DK:2 * DK], 1.0)
                        split_projection(2, 0)
                nc.vector.memset(normal_context[:, :], 0.0)
                for h in range(NH):
                    maximum(0, h)
                    if h % HALF == HALF - 1:
                        for part in range(2):
                            split_maxima(0, h // HALF, part)

            def slot(s, before, ffn, ahead1, ahead2, ahead3):
                b, r, _ = s.batch(0)
                b1 = s.batch(1)[0]
                for h in range(NH):
                    if h == 1 and before:
                        normalise(b - 1, 1)
                    if ahead1:
                        maximum(b1, h)
                    if h == 0 and before:
                        normalise(b - 1, 0)
                    if h == 1 and before:
                        normalise(b - 1, 2)
                    if ffn and s.odd and h < UP_FROM:
                        hid_high(s.pair, h + NH - 1 - UP_FROM)
                    if h == 1 and before:
                        normalise(b - 1, 3)
                    if ahead1 and h % HALF == HALF - 1:
                        split_maxima(b1, h // HALF, 0)
                    if h in (2, 3, 4) and ahead3:
                        b3, r3, _ = s.batch(3)
                        split_projection(b3, r3 % 2, (h - 2,))
                    if ffn and not s.odd and h > UP_FROM:
                        hid_high(s.pair, h - 1 - UP_FROM)
                    if ahead1 and h % HALF == HALF - 1:
                        split_maxima(b1, h // HALF, 1)
                    if h == 3 and before:
                        o_low(b - 1, ((r - 1) % RING) // 2, (r - 1) % 2)
                    if ffn and s.odd and h == UP_FROM - 1:
                        hid_high(s.pair, HT - 1)
                if isinstance(b, int) and b == 0:
                    dve.wait_ge(scales_loaded, 48)
                    nc.vector.tensor_scalar(out_scale[:, :], down_sc[:, :], out_sc[:, 0:1], None,
                                            ALU.mult).then_inc(scale_made, 1)
                    dve.wait_ge(scale_made, 1)
                if ffn and s.odd:
                    scale_out(s.pair)

            def last():
                for step in range(4):
                    normalise(B - 1, step)
                o_low(B - 1, 1, 1)
                for t in range(HT):
                    hid_high(B // 2 - 1, t)
                scale_out(B // 2 - 1)

            pipeline(dve, first, slot, last)


def kernel(x, cond_2048, L0_cond_Wq, L0_cond_Wo, L0_ffn_up_weight, L0_ffn_down_weight, L0_ffn_up_scale,
           L0_ffn_down_scale, L0_ffn_output_scale):
    import numpy as np
    import concourse.bacc as bacc
    from concourse import mybir as mb
    from concourse.bass_utils import run_bass_kernel_spmd

    nc = bacc.Bacc("TRN2", target_bir_lowering=False, num_devices=1)
    wq_t = np.asarray(L0_cond_Wq).T
    laid = {
        "x": np.asarray(x),
        "mask": np.asarray(cond_2048),
        "wq_by_head": wq_t,
        "wq_by_dim": wq_t.reshape(D, NH, DK).transpose(0, 2, 1).reshape(D, D),
        "wo_t": np.asarray(L0_cond_Wo).T,
        "up_t": np.asarray(L0_ffn_up_weight).T,
        "down_t": np.asarray(L0_ffn_down_weight).T,
        "up_scale": np.asarray(L0_ffn_up_scale).reshape(HT, P).T,
        "down_scale": np.asarray(L0_ffn_down_scale),
        "output_scale": np.asarray(L0_ffn_output_scale),
    }
    laid = {f"in_{k}": np.ascontiguousarray(v) for k, v in laid.items()}
    args = [nc.dram_tensor(k, v.shape, mb.dt.from_np(v.dtype), kind="ExternalInput").ap() for k, v in laid.items()]
    out = nc.dram_tensor("out", (B, D, T), F32, kind="ExternalOutput").ap()
    attention_ffn(nc, *args, out)
    r = run_bass_kernel_spmd(nc, [laid], core_ids=[0])
    return r.results[0]["out"]
```

```python
from contextlib import ExitStack

import concourse.bass as bass
import numpy as np
from concourse import mybir

F32 = mybir.dt.float32
F32R = mybir.dt.float32r
BF16 = mybir.dt.bfloat16
ACT = mybir.ActivationFunctionType
ALU = mybir.AluOpType
AX_X = mybir.AxisListType.X

B, D, T = 16, 128, 256
NH = 8
DK = D // NH
HID = 1024
P = 128
TT = T // P
HT = HID // P
HALF = NH // 2
SCALE = DK ** -0.5
NEG = -1e30 / SCALE
TWO_ONES = float(np.array([0x3F803F80], np.uint32).view(np.float32)[0])
BLOCKS = 2 * T // 32
HU = HT // 2
RING = 4
STACK_LOADS = 7

UP_AT = {7: 0, 8: 1, 10: 2, 11: 3}
DOWN_AT = {14: [(0, 0)], 15: [(0, 1), (0, 2)], 16: [(0, 3), (1, 0)], 18: [(1, 1), (1, 2)], 19: [(1, 3)]}

ROW_MID, ROW_HI, ROW_R, ROW_LO, ROW_NEG = 0, DK, 2 * DK, 2 * DK + 1, 3 * DK + 1
ROWS = 3 * DK + 2
K_MASKED = 6 * DK + 1
K_ALL = K_MASKED + 2


class Slot:

    def __init__(self, turn, j):
        self.turn, self.j = turn, j
        self.b = turn * RING + (2 + j)
        self.odd = j % 2 == 1

    def of_parity(self, d):
        return self.turn * 2 + (2 + self.j + d) // 2

    def ffn(self, h):
        k = h + NH if self.odd else h if h >= NH // 2 else h + 2 * NH
        n = self.j // 2 - (k >= 2 * NH)
        return self.turn * 2 + n, n % 2, k

    def batch(self, d):
        n = 2 + self.j + d
        return self.turn * RING + n, n % RING, self.turn + n // RING


def attention_ffn(nc, x, mask, wq_by_head, wq_by_dim, wo_t, up_t, down_t, up_scale, down_scale,
                  output_scale, out):
    parts = nc.dram_tensor("parts_dram", (B + 1, ROWS, NH * T), BF16, kind="Internal").ap()
    ctx = ExitStack()
    with ctx:
        def sb(name, shape, dt=F32):
            return ctx.enter_context(nc.sbuf_tensor(name, shape, dt))

        def pb(name):
            return ctx.enter_context(nc.psum_tensor(name, [P, 512], F32))

        def sem(name):
            return ctx.enter_context(nc.semaphore(name))

        x_all = sb("x_all", [P, B + 2, T])
        mask_first = sb("mask_first", [P, 2, T])
        mask_all = sb("mask_all", [P, B + 2, T], BF16)
        out_all = sb("out_all", [P, B, T])
        wq_h = sb("wq_h", [P, D])
        wq_d = sb("wq_d", [P, D])
        wo = sb("wo", [P, D])
        up_raw = sb("up_raw", [P, TT, HID])
        down_raw = sb("down_raw", [P, HT, T])
        up_sign = sb("up_sign", [P, TT, HID], F32R)
        down_sign = sb("down_sign", [P, HT, T], F32R)
        up_sc = sb("up_sc", [P, HT])
        down_sc = sb("down_sc", [P, T])
        out_sc = sb("out_sc", [P, 1])
        out_scale = sb("out_scale", [P, T])
        ident = sb("ident", [P, P], BF16)
        mask16 = sb("mask16", [B, T])
        r16 = sb("r16", [B, T], BF16)
        neg16 = sb("neg16", [B, T], BF16)
        x_masked = [sb(f"x_masked{i}", [P, T]) for i in range(2)]
        x_copy = [sb(f"x_copy{i}", [P, T]) for i in range(2)]
        q_parts = [sb(f"q_parts{i}", [P, 3, T], BF16) for i in range(2)]
        q_rest = sb("q_rest", [P, T])
        key_stack = [sb(f"key_stack{i}", [P, NH, T], BF16) for i in range(RING)]
        query_stack = [sb(f"query_stack{i}", [P, NH, T], BF16) for i in range(RING)]
        v_ones = [sb(f"v_ones{i}", [P, TT, NH, 32]) for i in range(RING)]
        maxima = sb("maxima", [P, 2, HALF, TT])
        neg_max = sb("neg_max", [P, 2, 2, HALF * TT], BF16)
        neg_max_rows = [sb(f"neg_max_rows{i}", [2 * HALF * TT, P], BF16) for i in range(2)]
        probs = sb("probs", [P, NH, TT * T])
        turned_context = sb("turned_context", [P, 2 * T])
        inverse_sums = sb("inverse_sums", [P, BLOCKS])
        normal_context = sb("normal_context", [P, T])
        context = sb("context", [P, T])
        o_hi = [sb(f"o_hi{i}", [P, TT, 2, D], F32R) for i in range(2)]
        o_lo = [sb(f"o_lo{i}", [P, TT, 2, D], F32R) for i in range(2)]
        hidden = sb("hidden", [P, HT, 2 * D])
        hid_hi = sb("hid_hi", [P, HT, 2 * D], F32R)
        hid_lo = sb("hid_lo", [P, HT, 2 * D], F32R)

        ps_exp = [pb(f"ps_exp{i}") for i in range(2)]
        ps_max = [pb(f"ps_max{i}") for i in range(2)]
        ps_ctx = pb("ps_ctx")
        ps_turn = pb("ps_turn")
        ps_up = pb("ps_up")
        ps_down = pb("ps_down")
        ps_neg_max = ps_turn[0:2 * HALF * TT, 0:P // 2].bitcast(BF16)

        weights_loaded, wo_loaded = sem("weights_loaded"), sem("wo_loaded")
        x_first, x_second, x_rest = sem("x_first"), sem("x_second"), sem("x_rest")
        mask_loaded, mask_stored = sem("mask_loaded"), sem("mask_stored")
        up_loaded, down_loaded, scales_loaded = sem("up_loaded"), sem("down_loaded"), sem("scales_loaded")
        parts_stored = [sem(f"parts_stored{i}") for i in range(2)]
        stack_loaded = [sem(f"stack_loaded{i}") for i in range(RING)]
        max_loaded = [sem(f"max_loaded{i}") for i in range(2)]
        out_stored = sem("out_stored")
        ident_zeroed, ident_made = sem("ident_zeroed"), sem("ident_made")
        x_masked_ready, x_copied = sem("x_masked_ready"), sem("x_copied")
        hid_lo_done, out_ready = sem("hid_lo_done"), sem("out_ready")
        q_projected, v_projected = sem("q_projected"), sem("v_projected")
        max_scored, exp_scored = sem("max_scored"), sem("exp_scored")
        max_turned, attended, out_projected = sem("max_turned"), sem("attended"), sem("out_projected")
        up_done, down_done = sem("up_done"), sem("down_done")
        signs_made = sem("signs_made")
        q_hi_done, v_done, max_copied = sem("q_hi_done"), sem("v_done"), sem("max_copied")
        exp_done, o_hi_done = sem("exp_done"), sem("o_hi_done")
        relu_done, hid_hi_done = sem("relu_done"), sem("hid_hi_done")
        constants_set, mask_rows_made = sem("constants_set"), sem("mask_rows_made")
        scale_made = sem("scale_made")
        q_rest_done, q_mid_done, q_lo_done = sem("q_rest_done"), sem("q_mid_done"), sem("q_lo_done")
        maxed, max_hi_done, max_split = sem("maxed"), sem("max_hi_done"), sem("max_split")
        context_turned, inverted, normalised = sem("context_turned"), sem("inverted"), sem("normalised")
        context_done, o_lo_done = sem("context_done"), sem("o_lo_done")
        scaled, last_hi_done, last_lo_done = sem("scaled"), sem("last_hi_done"), sem("last_lo_done")
        last_scaled, last_summed, last_stored = sem("last_scaled"), sem("last_summed"), sem("last_stored")

        block = ctx.enter_context(nc.Block())

        up_bank = [ps_down, ps_up] * 2
        last_up = [ps_up, ps_ctx, ps_max[0], ps_max[1]]
        last_down = ps_exp
        on_gpsimd = (1,)

        def pipeline(engine, first, slot, last):
            early, late, whole = range(NH // 2), range(NH // 2, NH), range(NH)
            first()
            slot(Slot(0, -2), whole, before=False, ffn=False, ahead1=True, ahead=True)
            slot(Slot(0, -1), whole, before=True, ffn=False, ahead1=True, ahead=True)
            slot(Slot(0, 0), early, before=True, ffn=False, ahead1=True, ahead=True)
            with engine.Fori(0, (B - RING) // RING) as turn:
                slot(Slot(turn, 0), late, before=True, ffn=True, ahead1=True, ahead=True)
                for j in range(1, RING):
                    slot(Slot(turn, j), whole, before=True, ffn=True, ahead1=True, ahead=True)
                slot(Slot(turn, RING), early, before=True, ffn=True, ahead1=True, ahead=True)
            end = (B - RING) // RING
            slot(Slot(end, 0), late, before=True, ffn=True, ahead1=True, ahead=False)
            slot(Slot(end, 1), whole, before=True, ffn=True, ahead1=False, ahead=False)
            last()

        @block.sync
        def _(sp):
            def load_parts(b, r):
                def rows(at, n, twice=False):
                    src = parts[b, at:at + n, :]
                    if twice:
                        src = bass.AP(src.tensor, src.offset, [[0, 2], [NH * T, n], [1, NH * T]])
                    return src
                key, query, done = key_stack[r], query_stack[r], stack_loaded[r]
                sp.dma_start(key[0:2 * DK, :, :], rows(ROW_MID, DK, True)).then_inc(done, 16)
                sp.dma_start(query[0:4 * DK, :, :], rows(ROW_MID, 2 * DK, True)).then_inc(done, 16)
                sp.dma_start(key[2 * DK:4 * DK, :, :], rows(ROW_HI, DK, True)).then_inc(done, 16)
                sp.dma_start(key[4 * DK:5 * DK, :, :], rows(ROW_HI, DK)).then_inc(done, 16)
                sp.dma_start(query[4 * DK:5 * DK, :, :], rows(ROW_LO, DK)).then_inc(done, 16)
                sp.dma_start(key[5 * DK:K_MASKED, :, :], rows(ROW_LO, DK + 1)).then_inc(done, 16)
                sp.dma_start(query[5 * DK:K_MASKED, :, :], rows(ROW_HI, DK + 1)).then_inc(done, 16)

            def store_parts(b, i):
                dst = parts[b, 0:2 * DK, :].rearrange("(s d) (h t) -> (d h) s t", s=2, h=NH)
                sp.wait_ge(q_hi_done, b + 1)
                sp.wait_ge(q_mid_done, b + 1)
                sp.dma_start(dst, q_parts[i][:, 0:2, :]).then_inc(parts_stored[i], 16)
                dst = parts[b, ROW_LO:ROW_LO + DK, :].rearrange("d (h t) -> (d h) t", h=NH)
                sp.wait_ge(q_lo_done, b + 1)
                sp.dma_start(dst, q_parts[i][:, 2, :]).then_inc(parts_stored[i], 16)

            def load_maxima(b, r, half):
                sp.wait_ge(max_copied, b * 2 + (half + 1))
                sp.dma_start(query_stack[r][K_MASKED:K_ALL, half * HALF:(half + 1) * HALF, :],
                             neg_max_rows[half][:, :]).then_inc(max_loaded[half], 16)

            def load_x(at, n, done):
                sp.dma_start(x_all[:, at:at + n, :], x[at:at + n].rearrange("b p t -> p b t")).then_inc(done, 16)

            def load_mask(at, n, done):
                sp.dma_start(mask_all[:, at:at + n, :],
                             parts[at:at + n, ROW_R, 0:T].partition_broadcast(P)).then_inc(done, 16)

            def first():
                load_x(0, 2, x_first)
                sp.dma_start(mask_first[:, :, :], mask[0:2, :].partition_broadcast(P)).then_inc(x_first, 16)
                sp.dma_start(wq_d[:, :], wq_by_dim).then_inc(weights_loaded, 16)
                sp.dma_start(mask16[:, :], mask).then_inc(mask_loaded, 16)
                sp.dma_start(wq_h[:, :], wq_by_head).then_inc(weights_loaded, 16)
                load_x(2, 6, x_second)
                sp.wait_ge(mask_rows_made, 1)
                for row, rows in ((ROW_R, r16), (ROW_NEG, neg16)):
                    src = rows[:, :].rearrange("b (a t) -> b a t", a=1).broadcast_to([B, NH, T])
                    sp.dma_start(parts[0:B, row, :].rearrange("b (h t) -> b h t", h=NH), src).then_inc(mask_stored, 16)
                store_parts(0, 0)
                sp.wait_ge(mask_stored, 2 * 16)
                load_mask(2, 6, x_second)
                store_parts(1, 1)
                sp.wait_ge(constants_set, RING)
                sp.wait_ge(parts_stored[0], 32)
                load_parts(0, 0)
                sp.wait_ge(parts_stored[1], 32)
                store_parts(2, 0)
                load_parts(1, 1)
                load_maxima(0, 0, 0)
                sp.wait_ge(parts_stored[0], 64)
                load_parts(2, 2)

            def slot(s, steps, before, ffn, ahead1, ahead):
                b, r, _ = s.batch(0)
                if 0 in steps:
                    load_maxima(b, r, 1)
                if isinstance(b, int) and b < 2:
                    load_weights(b, 0)
                if NH - 1 in steps:
                    if ahead and not (isinstance(b, int) and b == 0):
                        b2, r2, _ = s.batch(2)
                        sp.wait_ge(parts_stored[r2 % 2], s.of_parity(2) * 32 + 32)
                        load_parts(b2, r2)
                    if ahead1:
                        b1, r1, _ = s.batch(1)
                        load_maxima(b1, r1, 0)
                    if isinstance(b, int) and b < 2:
                        load_weights(b, 1)
                    if ahead:
                        b3, r3, _ = s.batch(3)
                        store_parts(b3, r3 % 2)
                    if isinstance(b, int) and b == 1:
                        load_mask(8, 8, x_rest)
                if isinstance(b, int) and b == 2 and 0 in steps:
                    load_x(8, 8, x_rest)

            def load_weights(which, half):
                if which == 0:
                    sp.dma_start(up_raw[:, half, :], up_t[half * P:(half + 1) * P, :]).then_inc(up_loaded, 16)
                    if half == 1:
                        sp.dma_start(wo[:, :], wo_t).then_inc(wo_loaded, 16)
                        sp.dma_start(up_sc[:, :], up_scale).then_inc(scales_loaded, 16)
                        sp.dma_start(down_sc[:, :], down_scale.partition_broadcast(P)).then_inc(scales_loaded, 16)
                        sp.dma_start(out_sc[:, :], output_scale.partition_broadcast(P)).then_inc(scales_loaded, 16)
                else:
                    rows = down_t[half * (HID // 2):(half + 1) * (HID // 2), :]
                    sp.dma_start(down_raw[:, half * HU:(half + 1) * HU, :],
                                 rows.rearrange("(k p) n -> p k n", p=P)).then_inc(down_loaded, 16)

            def last():
                for b in (B - 2, B - 1):
                    sp.wait_ge(last_summed, b - B + 3)
                    sp.dma_start(out[b], out_all[:, b, :]).then_inc(last_stored, 16)
                sp.wait_ge(last_stored, 2 * 16)
                sp.wait_ge(parts_stored[0], 32 * (B // 2 + 1))

            pipeline(sp, first, slot, last)

        @block.gpsimd
        def _(pool):
            def mask_x(b, i, masks):
                nc.gpsimd.tensor_tensor(x_masked[i][:, :], x_all[:, b, :], masks[:, b, :],
                                        ALU.mult).then_inc(x_masked_ready, 1)

            def copy_x(b, i):
                nc.gpsimd.tensor_copy(x_copy[i][:, :], x_all[:, b, :]).then_inc(x_copied, 1)

            def first():
                nc.gpsimd.memset(x_all[:, B:B + 2, :], 0.0)
                nc.gpsimd.memset(mask_all[:, B:B + 2, :], 0.0)
                nc.gpsimd.memset(ident[:, :], 0.0).then_inc(ident_zeroed, 1)
                pool.wait_ge(ident_zeroed, 1)
                nc.gpsimd.affine_select(out=ident[:, :], in_=ident[:, :], compare_op=ALU.not_equal, fill=1.0,
                                        base=0, pattern=[[-1, P]], channel_multiplier=1).then_inc(ident_made, 1)
                pool.wait_ge(x_first, 32)
                mask_x(0, 0, mask_first)
                mask_x(1, 1, mask_first)
                copy_x(0, 0)
                copy_x(1, 1)
                pool.wait_ge(x_second, 32)
                pool.wait_ge(q_projected, 2)
                mask_x(2, 0, mask_all)
                mask_x(3, 1, mask_all)
                pool.wait_ge(v_projected, 1)
                copy_x(2, 0)

            def hid_low(u):
                nc.gpsimd.tensor_tensor(hid_lo[:, 2 * u:2 * u + 2, :], hidden[:, 2 * u:2 * u + 2, :],
                                        hid_hi[:, 2 * u:2 * u + 2, :], ALU.subtract).then_inc(hid_lo_done, 1)

            def residual(pair):
                pool.wait_ge(scaled, pair + 1)
                o = out_all[:, bass.ds(pair * 2, 2), :]
                nc.gpsimd.tensor_tensor(o, o, x_all[:, bass.ds(pair * 2, 2), :], ALU.add).then_inc(out_ready, 1)
                pool.wait_ge(out_ready, pair + 1)
                pool.dma_start(out[bass.ds(pair * 2, 2)].rearrange("b p t -> p b t"), o).then_inc(out_stored, 16)

            def slot(s, steps, before, ffn, ahead1, ahead):
                b = s.b
                if 0 in steps and not s.odd and ffn:
                    residual(s.ffn(0)[0])
                if isinstance(b, int) and b == 2 and 0 in steps:
                    pool.wait_ge(x_rest, 2 * 16)
                if NH - 1 in steps and ahead:
                    b3, r3, _ = s.batch(3)
                    b4, r4, _ = s.batch(4)
                    pool.wait_ge(v_projected, b + 2)
                    pool.wait_ge(q_projected, b + 3)
                    mask_x(b4, r4 % 2, mask_all)
                    copy_x(b3, r3 % 2)
                if NH - 1 in steps and s.odd and ffn:
                    for u in range(HU):
                        pool.wait_ge(hid_hi_done, s.ffn(0)[0] * HU + (u + 1))
                        hid_low(u)

            def last():
                residual(B // 2 - 2)
                for u in on_gpsimd:
                    pool.wait_ge(last_hi_done, u + 1)
                    hid_low(u)
                pool.wait_ge(out_stored, 16 * (B // 2 - 1))

            pipeline(pool, first, slot, last)

        @block.tensor
        def _(pe):
            def project_q(b, i, bank=ps_up):
                pe.wait_ge(x_masked_ready, b + 1)
                nc.tensor.matmul(bank[:, 0:T], wq_d[:, :], x_masked[i][:, :],
                                 start=True, stop=True).then_inc(q_projected, 1)

            def project_v(b, i):
                pe.wait_ge(x_copied, b + 1)
                if not (isinstance(b, int) and b == 0):
                    pe.wait_ge(v_done, b)
                for t in range(TT):
                    mm = nc.tensor.matmul(ps_turn[:, t * D:(t + 1) * D], x_copy[i][:, t * P:(t + 1) * P],
                                          wq_h[:, :], start=True, stop=True)
                mm.then_inc(v_projected, 1)

            def score_max(b, r, uses, h):
                if h == 0:
                    pe.wait_ge(stack_loaded[r], (uses + 1) * (16 * STACK_LOADS))
                if not (isinstance(b, int) and b == 0 and h < 2):
                    pe.wait_ge(maxed, b * NH + (h - 1))
                for t in range(TT):
                    mm = nc.tensor.matmul(ps_max[h % 2][:, t * T:(t + 1) * T],
                                          query_stack[r][0:K_MASKED, h, t * P:(t + 1) * P],
                                          key_stack[r][0:K_MASKED, h, :], start=True, stop=True)
                mm.then_inc(max_scored, 1)

            def score_exp(b, r, h):
                if h % HALF == 0:
                    pe.wait_ge(max_loaded[h // HALF], b * 16 + 16)
                if not (isinstance(b, int) and b == 0 and h < 2):
                    pe.wait_ge(exp_done, b * NH + (h - 1))
                for t in range(TT):
                    mm = nc.tensor.matmul(ps_exp[h % 2][:, t * T:(t + 1) * T],
                                          key_stack[r][0:K_ALL, h, t * P:(t + 1) * P],
                                          query_stack[r][0:K_ALL, h, :], start=True, stop=True)
                mm.then_inc(exp_scored, 1)

            def turn_maxima(b, half):
                pe.wait_ge(max_split, b * 2 + (half + 1))
                nc.tensor.transpose(ps_neg_max, neg_max[:, half, :, :].rearrange("p s c -> p (s c)"),
                                    ident[:, :]).then_inc(max_turned, 1)

            def attend(b, r, half):
                pe.wait_ge(exp_done, b * NH + (half + 1) * HALF)
                if half == 0:
                    pe.wait_ge(v_done, b + 1)
                for t in range(TT):
                    for j in range(HALF):
                        h = half * HALF + j
                        mm = nc.tensor.matmul(ps_ctx[32 * j:32 * j + 32, half * T:(half + 1) * T],
                                              v_ones[r][:, t, h, :], probs[:, h, t * T:(t + 1) * T],
                                              start=t == 0, stop=t == TT - 1)
                mm.then_inc(attended, 1)

            def project_out(b):
                pe.wait_ge(context_done, b + 1)
                for t in range(TT):
                    mm = nc.tensor.matmul(ps_turn[:, t * D:(t + 1) * D], context[:, t * P:(t + 1) * P],
                                          wo[:, :], start=True, stop=True)
                mm.then_inc(out_projected, 1)

            def up(i, u, bank):
                for t in (2 * u, 2 * u + 1):
                    for n, (k, part) in enumerate((k, part) for k in range(TT) for part in (o_hi, o_lo)):
                        mm = nc.tensor.matmul(bank[:, t % 2 * 2 * D:(t % 2 + 1) * 2 * D],
                                              up_sign[:, k, t * P:(t + 1) * P],
                                              part[i][:, k, :, :].rearrange("p b s -> p (b s)"),
                                              start=n == 0, stop=n == 2 * TT - 1)
                mm.then_inc(up_done, 1)

            def down(bi, u, out_columns):
                for t in (2 * u, 2 * u + 1):
                    for part in (hid_hi, hid_lo):
                        mm = nc.tensor.matmul(out_columns, part[:, t, bi * D:(bi + 1) * D],
                                              down_sign[:, t, :], start=t == 0 and part is hid_hi,
                                              stop=t == HT - 1 and part is hid_lo)
                if u == HU - 1:
                    mm.then_inc(down_done, 1)

            def first():
                pe.wait_ge(weights_loaded, 32)
                project_q(0, 0, ps_up)
                project_q(1, 1, ps_down)
                project_v(0, 0)
                project_v(1, 1)
                pe.wait_ge(q_rest_done, 1)
                project_q(2, 0, ps_up)
                pe.wait_ge(ident_made, 1)
                for h in range(NH):
                    score_max(0, 0, 0, h)
                    if h == 5:
                        pe.wait_ge(v_done, 2)
                        turn_maxima(0, 0)

            def slot(s, steps, before, ffn, ahead1, ahead):
                b, r, _ = s.batch(0)
                b1, r1, uses1 = s.batch(1)
                b2, r2, _ = s.batch(2)
                b3, r3, _ = s.batch(3)
                for h in steps:
                    score_exp(b, r, h)
                    if ahead1:
                        score_max(b1, r1, uses1, h)
                    if h == 3 and ahead1:
                        pe.wait_ge(max_copied, b * 2 + 2)
                        project_v(b2, r2 % 2)
                    if h == (1 if ahead1 else 0):
                        if not (isinstance(b, int) and b < 2):
                            pe.wait_ge(o_lo_done, b - 1)
                        turn_maxima(b, 1)
                    if h == 1 and before:
                        attend(b - 1, (r - 1) % RING, 1)
                    if h == 4:
                        if before:
                            pe.wait_ge(context_turned, b)
                        attend(b, r, 0)
                        if ahead1:
                            pe.wait_ge(v_done, b2 + 1)
                            turn_maxima(b1, 0)
                    if h == 5 and ahead:
                        pe.wait_ge(q_rest_done, b3)
                        if ffn and s.odd:
                            pe.wait_ge(relu_done, s.ffn(h)[0] * HT + HT)
                        project_q(b3, r3 % 2)
                    if h == 5 and before:
                        if isinstance(b, int) and b == 1:
                            pe.wait_ge(wo_loaded, 16)
                        if ahead1:
                            pe.wait_ge(max_copied, b * 2 + 3)
                        project_out(b - 1)
                    if ffn:
                        pair, i, k = s.ffn(h)
                        if k in UP_AT:
                            u = UP_AT[k]
                            if u == 0:
                                pe.wait_ge(o_lo_done, pair * 2 + 2)
                            if u == 1 and ahead:
                                pe.wait_ge(q_rest_done, b3)
                            if u >= 2:
                                pe.wait_ge(relu_done, pair * HT + 2 * u - 2)
                            up(i, u, up_bank[u])
                        for bi, u in DOWN_AT.get(k, ()):
                            if (bi, u) == (0, 0):
                                pe.wait_ge(relu_done, pair * HT + HT - 2)
                            if bi == 0:
                                pe.wait_ge(hid_lo_done, pair * HU + (u + 1))
                            down(bi, u, ps_down[:, bi * T:(bi + 1) * T])
                if isinstance(b, int) and b in (1, 2) and 0 in steps:
                    pe.wait_ge(signs_made, 4 * b)

            def last():
                attend(B - 1, (B - 1) % RING, 1)
                left = [unit for k in range(2 * NH, 2 * NH + NH // 2) for unit in DOWN_AT.get(k, ())]
                for n, (bi, u) in enumerate(left):
                    if n == len(left) // 2:
                        pe.wait_ge(o_lo_done, B - 1)
                        project_out(B - 1)
                    if bi == 0:
                        pe.wait_ge(hid_lo_done, (B // 2 - 2) * HU + (u + 1))
                    down(bi, u, ps_down[:, bi * T:(bi + 1) * T])
                pe.wait_ge(o_lo_done, B)
                for u in range(HU):
                    up(1, u, last_up[u])
                for bi in range(2):
                    for u in range(HU):
                        if bi == 0 and u in on_gpsimd:
                            pe.wait_ge(hid_lo_done, (B // 2 - 1) * HU + sum(v <= u for v in on_gpsimd))
                        if bi == 0 and u not in on_gpsimd:
                            pe.wait_ge(last_lo_done, sum(v not in on_gpsimd for v in range(u + 1)))
                        down(bi, u, last_down[bi][:, 0:T])

            pipeline(pe, first, slot, last)

        @block.scalar
        def _(act):
            def q_high(b, i, stores, bank=ps_up):
                act.wait_ge(q_projected, b + 1)
                if stores is not None:
                    act.wait_ge(parts_stored[i], stores * 32)
                nc.scalar.copy(q_parts[i][:, 1, :], bank[:, 0:T]).then_inc(q_hi_done, 1)

            def values(b, r):
                act.wait_ge(v_projected, b + 1)
                nc.scalar.copy(v_ones[r][:, :, :, 0:DK],
                               ps_turn[:, 0:T].rearrange("p (t h d) -> p t h d", t=TT, h=NH)).then_inc(v_done, 1)

            def copy_maxima(b, half):
                act.wait_ge(max_turned, b * 2 + (half + 1))
                nc.scalar.copy(neg_max_rows[half][:, :], ps_neg_max).then_inc(max_copied, 1)

            def exps(b, h):
                act.wait_ge(exp_scored, b * NH + (h + 1))
                if h % HALF == 0 and not (isinstance(b, int) and b == 0):
                    act.wait_ge(attended, b * 2 + (h // HALF - 1))
                nc.scalar.activation(probs[:, h, :], ps_exp[h % 2][:, :], ACT.Exp, scale=SCALE).then_inc(exp_done, 1)

            def o_high(b, pair_buf, bi):
                act.wait_ge(out_projected, b + 1)
                nc.scalar.copy(o_hi[pair_buf][:, :, bi, :],
                               ps_turn[:, 0:T].rearrange("p (t d) -> p t d", t=TT)).then_inc(o_hi_done, 1)

            def relu(pair, u, bank):
                act.wait_ge(up_done, pair * HU + (u + 1))
                for t in (2 * u, 2 * u + 1):
                    nc.scalar.activation(hidden[:, t, :], bank[:, t % 2 * 2 * D:(t % 2 + 1) * 2 * D], ACT.Relu,
                                         scale=up_sc[:, t:t + 1]).then_inc(relu_done, 1)

            def hid_high(pair, u):
                act.wait_ge(relu_done, pair * HT + (2 * u + 2))
                nc.scalar.copy(hid_hi[:, 2 * u:2 * u + 2, :], hidden[:, 2 * u:2 * u + 2, :]).then_inc(hid_hi_done, 1)

            def slot(s, steps, before, ffn, ahead1, ahead):
                b, r, _ = s.batch(0)
                b2, r2, _ = s.batch(2)
                for h in steps:
                    exps(b, h)
                    if h == 3 and ahead1:
                        values(b2, r2)
                    if h == (1 if ahead1 else 0):
                        copy_maxima(b, 1)
                    if h == 4 and ahead1:
                        copy_maxima(s.batch(1)[0], 0)
                    if h == 5 and ahead:
                        b3, r3, _ = s.batch(3)
                        q_high(b3, r3 % 2, s.of_parity(3))
                    if h == 5 and before:
                        o_high(b - 1, ((r - 1) % RING) // 2, (r - 1) % 2)
                    if ffn:
                        pair, i, k = s.ffn(h)
                        if k - 1 in UP_AT:
                            hid_high(pair, UP_AT[k - 1])
                        if k in UP_AT:
                            relu(pair, UP_AT[k], up_bank[UP_AT[k]])
                    if isinstance(b, int) and b == 1 and h < 4:
                        act.wait_ge(up_loaded, 32)
                        k, n = h // 2, slice(h % 2 * (HID // 2), (h % 2 + 1) * (HID // 2))
                        nc.scalar.sign(up_sign[:, k, n], up_raw[:, k, n]).then_inc(signs_made, 1)
                    if isinstance(b, int) and b == 2 and h < 4:
                        act.wait_ge(down_loaded, 32)
                        k = slice(2 * h, 2 * h + 2)
                        nc.scalar.sign(down_sign[:, k, :], down_raw[:, k, :]).then_inc(signs_made, 1)
                if isinstance(b, int) and b == 1:
                    act.wait_ge(scales_loaded, 48)

            def last():
                o_high(B - 1, 1, 1)
                for u in range(HU):
                    relu(B // 2 - 1, u, last_up[u])

            def first():
                q_high(0, 0, None, ps_up)
                q_high(1, 1, None, ps_down)
                values(0, 0)
                values(1, 1)
                q_high(2, 0, 1, ps_up)
                copy_maxima(0, 0)

            pipeline(act, first, slot, last)

        @block.vector
        def _(dve):
            def split_projection(b, i, stages=(0, 1, 2), bank=ps_up):
                if 0 in stages:
                    if not (isinstance(b, int) and b == 0):
                        dve.wait_ge(q_lo_done, b)
                    dve.wait_ge(q_hi_done, b + 1)
                    nc.vector.tensor_tensor(q_rest[:, :], bank[:, 0:T], q_parts[i][:, 1, :],
                                            ALU.subtract).then_inc(q_rest_done, 1)
                if 1 in stages:
                    dve.wait_ge(q_rest_done, b + 1)
                    nc.vector.tensor_copy(q_parts[i][:, 0, :], q_rest[:, :]).then_inc(q_mid_done, 1)
                if 2 in stages:
                    dve.wait_ge(q_mid_done, b + 1)
                    nc.vector.tensor_tensor(q_parts[i][:, 2, :], q_rest[:, :], q_parts[i][:, 0, :],
                                            ALU.subtract).then_inc(q_lo_done, 1)

            def maximum(b, h):
                dve.wait_ge(max_scored, b * NH + (h + 1))
                nc.vector.reduce_max(maxima[:, h // HALF, h % HALF, :],
                                     ps_max[h % 2][:, :].rearrange("p (t k) -> p t k", t=TT),
                                     AX_X).then_inc(maxed, 1)

            def split_maxima(b, half, part):
                m = maxima[:, half, :, :].rearrange("p h t -> p (h t)")
                if part == 0:
                    dve.wait_ge(maxed, b * NH + (half + 1) * HALF)
                    nc.vector.tensor_scalar(neg_max[:, half, 0, :], m, -1.0, None, ALU.mult).then_inc(max_hi_done, 1)
                else:
                    dve.wait_ge(max_hi_done, b * 2 + (half + 1))
                    nc.vector.scalar_tensor_tensor(out=neg_max[:, half, 1, :], in0=m, scalar=-1.0,
                                                   in1=neg_max[:, half, 0, :], op0=ALU.mult,
                                                   op1=ALU.subtract).then_inc(max_split, 1)

            def normalise(b, step):
                turned = turned_context[:, :].rearrange("p (g n c) -> p g n c", g=2, c=32)
                if step == 0:
                    dve.wait_ge(attended, b * 2 + 2)
                    nc.vector.transpose(turned_context[:, :], ps_ctx[:, :]).then_inc(context_turned, 1)
                if step == 1:
                    dve.wait_ge(context_turned, b + 1)
                    nc.vector.reciprocal(inverse_sums[:, :],
                                         turned_context[:, :].rearrange("p (n c) -> p n c", c=32)[:, :, DK]
                                         ).then_inc(inverted, 1)
                if step == 2:
                    dve.wait_ge(inverted, b + 1)
                    inverse = inverse_sums[:, :].rearrange("p (g n a) -> p g n a", g=2, a=1)
                    nc.vector.tensor_tensor(normal_context[:, :].rearrange("p (n g c) -> p g n c", g=2, c=DK),
                                            turned[:, :, :, 0:DK],
                                            inverse.broadcast_to([P, 2, BLOCKS // 2, DK]),
                                            ALU.mult).then_inc(normalised, 1)
                if step == 3:
                    dve.wait_ge(normalised, b + 1)
                    nc.vector.transpose(context[:, :], normal_context[:, :]).then_inc(context_done, 1)

            def o_low(b, pair_buf, bi):
                dve.wait_ge(o_hi_done, b + 1)
                nc.vector.tensor_tensor(o_lo[pair_buf][:, :, bi, :],
                                        ps_turn[:, 0:T].rearrange("p (t d) -> p t d", t=TT),
                                        o_hi[pair_buf][:, :, bi, :], ALU.subtract).then_inc(o_lo_done, 1)

            def scale_out(pair):
                dve.wait_ge(down_done, pair * 2 + 2)
                nc.vector.tensor_tensor(out_all[:, bass.ds(pair * 2, 2), :],
                                        ps_down[:, :].rearrange("p (b t) -> p b t", b=2),
                                        out_scale[:, :].rearrange("p (a t) -> p a t", a=1).broadcast_to([P, 2, T]),
                                        ALU.mult).then_inc(scaled, 1)

            def first():
                for r in range(RING):
                    nc.vector.memset(key_stack[r][6 * DK:K_ALL, :, :].bitcast(F32), TWO_ONES).then_inc(constants_set, 1)
                dve.wait_ge(mask_loaded, 16)
                nc.vector.tensor_copy(r16[:, :], mask16[:, :])
                nc.vector.tensor_scalar(neg16[:, :], mask16[:, :], -NEG, NEG, ALU.mult,
                                        ALU.add).then_inc(mask_rows_made, 1)
                split_projection(0, 0, bank=ps_up)
                split_projection(1, 1, bank=ps_down)
                for v in v_ones:
                    nc.vector.memset(v[:, :, :, DK:2 * DK], 1.0)
                split_projection(2, 0, bank=ps_up)
                for h in range(NH):
                    maximum(0, h)
                    if h % HALF == HALF - 1:
                        for part in range(2):
                            split_maxima(0, h // HALF, part)

            def slot(s, steps, before, ffn, ahead1, ahead):
                b, r, _ = s.batch(0)
                b1 = s.batch(1)[0]
                b3, r3, _ = s.batch(3)
                for h in steps:
                    if h == 4 and before:
                        normalise(b - 1, 3)
                    if h == 6 and ahead:
                        split_projection(b3, r3 % 2, (0,))
                    if h == 6 and before:
                        o_low(b - 1, ((r - 1) % RING) // 2, (r - 1) % 2)
                    if ahead1:
                        maximum(b1, h)
                    if ahead1 and h % HALF == HALF - 1:
                        split_maxima(b1, h // HALF, 0)
                    if h == 2 and before:
                        normalise(b - 1, 0)
                    if h == 3 and before:
                        normalise(b - 1, 1)
                    if h == 6 and ahead:
                        split_projection(b3, r3 % 2, (1,))
                    if ahead1 and h % HALF == HALF - 1:
                        split_maxima(b1, h // HALF, 1)
                    if h == 3 and before:
                        normalise(b - 1, 2)
                    if h == 6 and ahead:
                        split_projection(b3, r3 % 2, (2,))
                    if h == 3 and not s.odd and ffn:
                        scale_out(s.ffn(h)[0])
                if isinstance(b, int) and b == 1:
                    dve.wait_ge(scales_loaded, 48)
                    nc.vector.tensor_scalar(out_scale[:, :], down_sc[:, :], out_sc[:, 0:1], None,
                                            ALU.mult).then_inc(scale_made, 1)
                    dve.wait_ge(scale_made, 1)

            def last():
                pair = B // 2 - 1
                for step in range(4):
                    normalise(B - 1, step)
                o_low(B - 1, 1, 1)
                scale_out(pair - 1)
                for u in range(HU):
                    tiles = slice(2 * u, 2 * u + 2)
                    dve.wait_ge(relu_done, pair * HT + (2 * u + 2))
                    nc.vector.tensor_copy(hid_hi[:, tiles, :], hidden[:, tiles, :]).then_inc(last_hi_done, 1)
                    if u not in on_gpsimd:
                        dve.wait_ge(last_hi_done, u + 1)
                        nc.vector.tensor_tensor(hid_lo[:, tiles, :], hidden[:, tiles, :], hid_hi[:, tiles, :],
                                                ALU.subtract).then_inc(last_lo_done, 1)
                for b in (B - 2, B - 1):
                    dve.wait_ge(down_done, b + 1)
                    nc.vector.tensor_tensor(out_all[:, b, :], last_down[b % 2][:, 0:T], out_scale[:, :],
                                            ALU.mult).then_inc(last_scaled, 1)
                    dve.wait_ge(last_scaled, b - B + 3)
                    nc.vector.tensor_tensor(out_all[:, b, :], out_all[:, b, :], x_all[:, b, :],
                                            ALU.add).then_inc(last_summed, 1)

            pipeline(dve, first, slot, last)


def kernel(x, cond_2048, L0_cond_Wq, L0_cond_Wo, L0_ffn_up_weight, L0_ffn_down_weight, L0_ffn_up_scale,
           L0_ffn_down_scale, L0_ffn_output_scale):
    import concourse.bacc as bacc
    from concourse import mybir as mb
    from concourse.bass_utils import run_bass_kernel_spmd

    nc = bacc.Bacc("TRN2", target_bir_lowering=False, num_devices=1)
    wq_t = np.asarray(L0_cond_Wq).T
    laid = {
        "x": np.asarray(x),
        "mask": np.asarray(cond_2048),
        "wq_by_head": wq_t,
        "wq_by_dim": wq_t.reshape(D, NH, DK).transpose(0, 2, 1).reshape(D, D),
        "wo_t": np.asarray(L0_cond_Wo).T.reshape(2, HALF, DK, D).transpose(1, 0, 2, 3).reshape(D, D),
        "up_t": np.asarray(L0_ffn_up_weight).T,
        "down_t": np.asarray(L0_ffn_down_weight).T,
        "up_scale": np.asarray(L0_ffn_up_scale).reshape(HT, P).T,
        "down_scale": np.asarray(L0_ffn_down_scale),
        "output_scale": np.asarray(L0_ffn_output_scale),
    }
    laid = {f"in_{k}": np.ascontiguousarray(v) for k, v in laid.items()}
    args = [nc.dram_tensor(k, v.shape, mb.dt.from_np(v.dtype), kind="ExternalInput").ap() for k, v in laid.items()]
    out = nc.dram_tensor("out", (B, D, T), F32, kind="ExternalOutput").ap()
    attention_ffn(nc, *args, out)
    r = run_bass_kernel_spmd(nc, [laid], core_ids=[0])
    return r.results[0]["out"]
```
